# Optimizing a Trainium2 kernel written in Bass

```python
import numpy as np
import jax
import jax.numpy as jnp

def _softmax(x, axis=-1):
    return jax.nn.softmax(x, axis=axis)
def _gelu(x):
    return jax.nn.gelu(x, approximate=True)
def _silu(x):
    return jax.nn.silu(x)
def _sigmoid(x):
    return jax.nn.sigmoid(x)
def _layernorm(x, axis=-1, eps=1e-5):
    m = jnp.mean(x, axis=axis, keepdims=True)
    v = jnp.var(x, axis=axis, keepdims=True)
    return (x - m) / jnp.sqrt(v + eps)
def _scatter_add(tgt, idx, src, axis=0):
    return tgt.at[idx].add(src)
def _segment_sum(src, seg, n):
    return jax.ops.segment_sum(src, seg, n)

kernel_name = 'mk_conv_seq_d2_conv_nchw512_579db4'

def setup_inputs(seed: int = 0):
    np.random.seed(seed)
    _w = jnp.asarray
    def _rec_inputs():
        import jax
        import jax.numpy as jnp
        _gk = jax.random.key(seed)
        x = -7.109e-05 + 0.9999 * jax.random.normal(jax.random.fold_in(_gk, 1), (8, 512, 128, 128), jnp.float32)
        return x
    x = _rec_inputs()
    def _L0_conv_setup():
        import jax, jax.numpy as jnp
        import numpy as np
        B, CH, H, W = (8, 512, 128, 128)
        K, N = (8, 2)
        KM_ITERS, EM_ITERS = (10, 10)
        EPS = 1e-06

        def _kmeans_labels(xs):
            c = xs.shape[0]
            init_idx = jnp.round(jnp.linspace(0.0, c - 1.0, K)).astype(jnp.int32)
            cent = xs[init_idx]
            x2 = (xs ** 2).sum(1, keepdims=True)
            for _ in range(KM_ITERS):
                d = x2 - 2.0 * (xs @ cent.T) + (cent ** 2).sum(1)[None, :]
                labels = jnp.argmin(d, axis=1)
                oh = jax.nn.one_hot(labels, K, dtype=xs.dtype)
                cnt = oh.sum(0)
                new_cent = oh.T @ xs / jnp.maximum(cnt, 1.0)[:, None]
                cent = jnp.where((cnt > 0.0)[:, None], new_cent, cent)
            d = x2 - 2.0 * (xs @ cent.T) + (cent ** 2).sum(1)[None, :]
            return jnp.argmin(d, axis=1)

        def _gmm_fit(data):
            b, P, k = data.shape
            pick = jnp.round(jnp.linspace(0.0, P - 1.0, N)).astype(jnp.int32)
            mu = data[:, pick, :]
            var = jnp.broadcast_to(data.var(axis=1, keepdims=True) + EPS, mu.shape)
            wts = jnp.full((b, N), 1.0 / N, dtype=data.dtype)
            log2pi = jnp.log(2.0 * jnp.pi).astype(data.dtype)
            for _ in range(EM_ITERS):
                diff2 = ((data[:, :, None, :] - mu[:, None, :, :]) ** 2 / var[:, None, :, :]).sum(-1)
                logdet = jnp.log(var).sum(-1)
                logp = -0.5 * (diff2 + logdet[:, None, :] + k * log2pi) + jnp.log(wts)[:, None, :]
                resp = jax.nn.softmax(logp, axis=2)
                Nk = resp.sum(1)
                mu = jnp.einsum('bpn,bpk->bnk', resp, data) / Nk[..., None]
                ex2 = jnp.einsum('bpn,bpk->bnk', resp, data ** 2) / Nk[..., None]
                var = jnp.maximum(ex2 - mu ** 2 + EPS, EPS)
                wts = Nk / P
            return (mu, var)

        def _bilinear_up_x2(x):
            b, c, h, w = x.shape

            def coords(n_in, n_out):
                s = jnp.linspace(0.0, n_in - 1.0, n_out)
                i0 = jnp.floor(s).astype(jnp.int32)
                i1 = jnp.minimum(i0 + 1, n_in - 1)
                return (i0, i1, (s - i0).astype(x.dtype))
            y0, y1, fy = coords(h, 2 * h)
            x0, x1, fx = coords(w, 2 * w)
            rows = x[:, :, y0, :] * (1.0 - fy)[None, None, :, None] + x[:, :, y1, :] * fy[None, None, :, None]
            return rows[:, :, :, x0] * (1.0 - fx) + rows[:, :, :, x1] * fx

        def _forward(sx, w_down, w_conv, w_up):
            c2 = sx.shape[1] // 2
            x = jax.lax.conv_general_dilated(sx, w_down, window_strides=(2, 2), padding=((1, 1), (1, 1)), feature_group_count=c2, dimension_numbers=('NCHW', 'OIHW', 'NCHW'))
            b, c, h, w = x.shape
            xx = jax.lax.stop_gradient(x[0].reshape(c, h * w))
            mn = xx.min(axis=1, keepdims=True)
            mx = xx.max(axis=1, keepdims=True)
            xs = (xx - mn) / jnp.maximum(mx - mn, 1e-12)
            labels = _kmeans_labels(xs)
            oh = jax.nn.one_hot(labels, K, dtype=xx.dtype)
            cnt = oh.sum(0)
            cl_mean = oh.T @ xx / jnp.maximum(cnt, 1.0)[:, None]
            v22 = cl_mean.std(axis=1)
            order = jnp.argsort(v22)
            inv = jnp.argsort(order)
            slabel = inv[labels]
            soh = jax.nn.one_hot(slabel, K, dtype=x.dtype)
            scnt = soh.sum(0)
            v5 = jnp.einsum('bchw,ck->bkhw', x, soh / jnp.maximum(scnt, 1.0)[None, :])
            wa = jax.lax.stop_gradient(v5.reshape(b, K, h * w).transpose(0, 2, 1))
            mu, var = _gmm_fit(wa)
            v6 = mu.transpose(0, 2, 1)
            v66 = var.transpose(0, 2, 1)
            box = jnp.take_along_axis(v6, jnp.argsort(v66, axis=2), axis=2)
            y = jax.nn.sigmoid(jnp.einsum('bkn,kn->bk', box, w_conv))
            gate = y[:, slabel]
            pre_up = gate[:, :, None, None] * x + x
            up = jnp.repeat(pre_up, 2, axis=1) * w_up[None, :, None, None]
            return _bilinear_up_x2(up) + sx
        key = jax.random.key(seed)
        k1, k2, k3, k4 = jax.random.split(key, 4)
        sx = jax.random.normal(k1, (B, CH, H, W), dtype=jnp.float32)
        w_down = jax.random.normal(k2, (CH // 2, 2, 3, 3), dtype=jnp.float32) * 0.1
        w_conv = jax.random.normal(k3, (K, N), dtype=jnp.float32) * 0.5
        w_up = jax.random.normal(k4, (CH,), dtype=jnp.float32) * 0.1
        return {'sx': sx, 'w_down': w_down, 'w_conv': w_conv, 'w_up': w_up}
    _L0_conv_all = _L0_conv_setup()
    _L0_conv_in = {k: v for k, v in _L0_conv_all.items() if k in ('w_down', 'w_conv', 'w_up', )}
    del _L0_conv_all

    def _L1_conv_setup():
        import jax, jax.numpy as jnp
        import numpy as np
        BN_EPS = 1e-05

        def relu6(v):
            return jnp.clip(v, 0.0, 6.0)
        key = jax.random.key(seed)
        ks = jax.random.split(key, 7)
        C, R = (512, 128)
        B, H, W = (8, 128, 128)
        x = jax.random.normal(ks[0], (B, C, H, W), dtype=jnp.float32)
        w_guide = jax.random.normal(ks[1], (R, C), dtype=jnp.float32) * (1.0 / np.sqrt(C))
        w_fuse = jax.random.normal(ks[2], (C, R), dtype=jnp.float32) * (1.0 / np.sqrt(R))
        bn_gamma = jax.random.normal(ks[3], (C,), dtype=jnp.float32) * 0.1 + 1.0
        bn_beta = jax.random.normal(ks[4], (C,), dtype=jnp.float32) * 0.1
        bn_mean = jax.random.normal(ks[5], (C,), dtype=jnp.float32) * 0.1
        bn_var = jax.random.uniform(ks[6], (C,), dtype=jnp.float32, minval=0.5, maxval=1.5)
        return {'x': x, 'w_guide': w_guide, 'w_fuse': w_fuse, 'bn_gamma': bn_gamma, 'bn_beta': bn_beta, 'bn_mean': bn_mean, 'bn_var': bn_var}
    _L1_conv_all = _L1_conv_setup()
    _L1_conv_in = {k: v for k, v in _L1_conv_all.items() if k in ('w_guide', 'w_fuse', 'bn_gamma', 'bn_beta', 'bn_mean', 'bn_var', )}
    del _L1_conv_all

    return {
        "x": x,
        "L0_conv_w_down": _L0_conv_in["w_down"],
        "L0_conv_w_conv": _L0_conv_in["w_conv"],
        "L0_conv_w_up": _L0_conv_in["w_up"],
        "L1_conv_w_guide": _L1_conv_in["w_guide"],
        "L1_conv_w_fuse": _L1_conv_in["w_fuse"],
        "L1_conv_bn_gamma": _L1_conv_in["bn_gamma"],
        "L1_conv_bn_beta": _L1_conv_in["bn_beta"],
        "L1_conv_bn_mean": _L1_conv_in["bn_mean"],
        "L1_conv_bn_var": _L1_conv_in["bn_var"],
    }

def reference(x, L0_conv_w_down, L0_conv_w_conv, L0_conv_w_up, L1_conv_w_guide, L1_conv_w_fuse, L1_conv_bn_gamma, L1_conv_bn_beta, L1_conv_bn_mean, L1_conv_bn_var):
    import jax
    import jax.numpy as jnp
    def _L0_conv_ref(sx, w_down, w_conv, w_up):
        import jax, jax.numpy as jnp
        import numpy as np
        B, CH, H, W = (8, 512, 128, 128)
        K, N = (8, 2)
        KM_ITERS, EM_ITERS = (10, 10)
        EPS = 1e-06

        def _kmeans_labels(xs):
            c = xs.shape[0]
            init_idx = jnp.round(jnp.linspace(0.0, c - 1.0, K)).astype(jnp.int32)
            cent = xs[init_idx]
            x2 = (xs ** 2).sum(1, keepdims=True)
            for _ in range(KM_ITERS):
                d = x2 - 2.0 * (xs @ cent.T) + (cent ** 2).sum(1)[None, :]
                labels = jnp.argmin(d, axis=1)
                oh = jax.nn.one_hot(labels, K, dtype=xs.dtype)
                cnt = oh.sum(0)
                new_cent = oh.T @ xs / jnp.maximum(cnt, 1.0)[:, None]
                cent = jnp.where((cnt > 0.0)[:, None], new_cent, cent)
            d = x2 - 2.0 * (xs @ cent.T) + (cent ** 2).sum(1)[None, :]
            return jnp.argmin(d, axis=1)

        def _gmm_fit(data):
            b, P, k = data.shape
            pick = jnp.round(jnp.linspace(0.0, P - 1.0, N)).astype(jnp.int32)
            mu = data[:, pick, :]
            var = jnp.broadcast_to(data.var(axis=1, keepdims=True) + EPS, mu.shape)
            wts = jnp.full((b, N), 1.0 / N, dtype=data.dtype)
            log2pi = jnp.log(2.0 * jnp.pi).astype(data.dtype)
            for _ in range(EM_ITERS):
                diff2 = ((data[:, :, None, :] - mu[:, None, :, :]) ** 2 / var[:, None, :, :]).sum(-1)
                logdet = jnp.log(var).sum(-1)
                logp = -0.5 * (diff2 + logdet[:, None, :] + k * log2pi) + jnp.log(wts)[:, None, :]
                resp = jax.nn.softmax(logp, axis=2)
                Nk = resp.sum(1)
                mu = jnp.einsum('bpn,bpk->bnk', resp, data) / Nk[..., None]
                ex2 = jnp.einsum('bpn,bpk->bnk', resp, data ** 2) / Nk[..., None]
                var = jnp.maximum(ex2 - mu ** 2 + EPS, EPS)
                wts = Nk / P
            return (mu, var)

        def _bilinear_up_x2(x):
            b, c, h, w = x.shape

            def coords(n_in, n_out):
                s = jnp.linspace(0.0, n_in - 1.0, n_out)
                i0 = jnp.floor(s).astype(jnp.int32)
                i1 = jnp.minimum(i0 + 1, n_in - 1)
                return (i0, i1, (s - i0).astype(x.dtype))
            y0, y1, fy = coords(h, 2 * h)
            x0, x1, fx = coords(w, 2 * w)
            rows = x[:, :, y0, :] * (1.0 - fy)[None, None, :, None] + x[:, :, y1, :] * fy[None, None, :, None]
            return rows[:, :, :, x0] * (1.0 - fx) + rows[:, :, :, x1] * fx

        def _forward(sx, w_down, w_conv, w_up):
            c2 = sx.shape[1] // 2
            x = jax.lax.conv_general_dilated(sx, w_down, window_strides=(2, 2), padding=((1, 1), (1, 1)), feature_group_count=c2, dimension_numbers=('NCHW', 'OIHW', 'NCHW'))
            b, c, h, w = x.shape
            xx = jax.lax.stop_gradient(x[0].reshape(c, h * w))
            mn = xx.min(axis=1, keepdims=True)
            mx = xx.max(axis=1, keepdims=True)
            xs = (xx - mn) / jnp.maximum(mx - mn, 1e-12)
            labels = _kmeans_labels(xs)
            oh = jax.nn.one_hot(labels, K, dtype=xx.dtype)
            cnt = oh.sum(0)
            cl_mean = oh.T @ xx / jnp.maximum(cnt, 1.0)[:, None]
            v22 = cl_mean.std(axis=1)
            order = jnp.argsort(v22)
            inv = jnp.argsort(order)
            slabel = inv[labels]
            soh = jax.nn.one_hot(slabel, K, dtype=x.dtype)
            scnt = soh.sum(0)
            v5 = jnp.einsum('bchw,ck->bkhw', x, soh / jnp.maximum(scnt, 1.0)[None, :])
            wa = jax.lax.stop_gradient(v5.reshape(b, K, h * w).transpose(0, 2, 1))
            mu, var = _gmm_fit(wa)
            v6 = mu.transpose(0, 2, 1)
            v66 = var.transpose(0, 2, 1)
            box = jnp.take_along_axis(v6, jnp.argsort(v66, axis=2), axis=2)
            y = jax.nn.sigmoid(jnp.einsum('bkn,kn->bk', box, w_conv))
            gate = y[:, slabel]
            pre_up = gate[:, :, None, None] * x + x
            up = jnp.repeat(pre_up, 2, axis=1) * w_up[None, :, None, None]
            return _bilinear_up_x2(up) + sx
        return _forward(sx, w_down, w_conv, w_up)

    def _L1_conv_ref(x, w_guide, w_fuse, bn_gamma, bn_beta, bn_mean, bn_var):
        import jax, jax.numpy as jnp
        import numpy as np
        BN_EPS = 1e-05

        def relu6(v):
            return jnp.clip(v, 0.0, 6.0)
        y = jnp.mean(x, axis=(2, 3))
        y = relu6(jnp.einsum('rc,bc->br', w_guide, y))
        y = jnp.einsum('cr,br->bc', w_fuse, y)
        inv_std = jax.lax.rsqrt(bn_var + BN_EPS)
        y = relu6((y - bn_mean) * inv_std * bn_gamma + bn_beta)
        return x + y[:, :, None, None]

    def _gn(v, G=32, eps=1e-5):
        B_, C_, H_, W_ = v.shape
        g = v.reshape(B_, G, C_ // G, H_, W_)
        m = jnp.mean(g, axis=(2, 3, 4), keepdims=True)
        s = jnp.var(g, axis=(2, 3, 4), keepdims=True)
        return ((g - m) / jnp.sqrt(s + eps)).reshape(v.shape)

    def _ln_c(v, eps=1e-6):
        m = jnp.mean(v, axis=1, keepdims=True)
        s = jnp.var(v, axis=1, keepdims=True)
        return (v - m) / jnp.sqrt(s + eps)

    def _ln_t(v, eps=1e-5):
        m = jnp.mean(v, axis=-1, keepdims=True)
        s = jnp.var(v, axis=-1, keepdims=True)
        return (v - m) / jnp.sqrt(s + eps)

    def _to_tokens(v):
        B_, C_, H_, W_ = v.shape
        return v.reshape(B_, C_, H_ * W_).transpose(0, 2, 1)
    def _from_tokens(t, like):
        B_, C_, H_, W_ = like.shape
        return t.transpose(0, 2, 1).reshape(B_, C_, H_, W_)

    x = _L0_conv_ref(x, L0_conv_w_down, L0_conv_w_conv, L0_conv_w_up)
    x = _L1_conv_ref(x, L1_conv_w_guide, L1_conv_w_fuse, L1_conv_bn_gamma, L1_conv_bn_beta, L1_conv_bn_mean, L1_conv_bn_var)
    return x


_drawn_inputs = setup_inputs


def setup_inputs(seed=0):
    import zlib

    import numpy as np

    out = dict(_drawn_inputs(seed))
    spreads = {}
    factors = {'L0_conv_w_conv': 8.0,
     'L1_conv_w_guide': 8.0,
     'L1_conv_w_fuse': 8.0,
     'L1_conv_bn_gamma': 8.0,
     'L1_conv_bn_var': 4.685}
    for name, (base, spread) in spreads.items():
        noise = np.random.default_rng([zlib.crc32(name.encode()), seed]).standard_normal(out[name].shape)
        drawn = base * np.exp(spread * noise) if base else spread * noise
        out[name] = jnp.asarray(drawn.astype(out[name].dtype))
    for name, factor in factors.items():
        out[name] = (out[name] * factor).astype(out[name].dtype)
    return out
```

```python
from contextlib import ExitStack

import concourse.bass as bass
import numpy as np
from concourse import mybir

F32 = mybir.dt.float32
BF16 = mybir.dt.bfloat16
ALU = mybir.AluOpType
ACT = mybir.ActivationFunctionType
AX = mybir.AxisListType
ds = bass.ds

P = 128
B, CH, H, W = 8, 512, 128, 128
HC, WC = H // 2, W // 2
PX = HC * WC
TILES = CH // 2 // P
XR = 16
CR = XR // 2
S = H // XR
U = S // 2
STEPS = TILES * S
CN = CR * WC
K, N = 8, 2
KM_ITERS, EM_ITERS = 10, 10
EPS, BN_EPS = 1e-6, 1e-5
CHUNKS = PX // P
BLK = 512
PAIR = 2 * WC

PE_TAPS = [(i, ky, kx) for ky in (1, 2) for kx in (1, 0, 2) for i in range(2)]
DVE_TAPS = [(i, 0, kx) for kx in (1, 0, 2) for i in range(2)]

C_ID, C_U, C_COEF, C_FIRST, C_LAST = 0, 128, 256, 384, 512
C_SEED, C_TRI, C_IOTA, C_PREF, C_ROWW = 640, 656, 720, 728, 736
C_ALL = 800

PS_CONV, PS_T, PS_UP, PS_SMALL = 0, 1, 3, 7
SM_SUM, SM_Y1, SM_Y2 = 256, 320, 328


def shape_constants():
    def coords(n_in, n_out):
        at = np.linspace(0.0, n_in - 1.0, n_out).astype(np.float32)
        low = np.floor(at).astype(np.int64)
        return low, np.minimum(low + 1, n_in - 1), (at - low.astype(np.float32)).astype(np.float32)

    c = np.zeros((P, C_ALL), np.float32)
    c[:, C_ID:C_ID + P] = np.eye(P)
    x0, x1, fx = coords(WC, W)
    u = np.zeros((WC, W), np.float32)
    for w in range(W):
        u[x0[w], w] += np.float32(1) - fx[w]
        u[x1[w], w] += fx[w]
    c[:, C_U:C_U + W] = np.concatenate([u, u])
    y0, _, fy = coords(HC, H)
    for y in range(H):
        s, r = divmod(y, XR)
        low = CR * s + (r + 1) // 2 - 1
        pos = C_COEF + XR * s + (r - 1) % XR
        wts = {int(y0[y]): np.float32(1) - fy[y], int(y0[y]) + 1: fy[y]}
        assert all(row in (low, low + 1) or not v for row, v in wts.items())
        c[:WC, pos] = wts.get(low, 0)
        c[WC:, pos] = wts.get(low + 1, 0)
    c[0, C_FIRST:C_FIRST + P] = 1
    c[P - 1, C_LAST:C_LAST + P] = 1
    for k, ch in enumerate(np.round(np.linspace(0.0, TILES * P - 1.0, K)).astype(np.int64)):
        c[ch % P, C_SEED + K * (ch // P) + k] = 1
    c[:, C_TRI:C_TRI + K * K] = np.tril(np.ones((K, K)), -1).reshape(-1)
    c[:, C_IOTA:C_IOTA + K] = np.arange(K)
    c[:, C_PREF:C_PREF + K] = np.arange(K, 0, -1)
    a = (2 * HC) / (HC - 0.5)
    row = np.full(HC, a)
    row[[0, -1]] *= 0.75
    c[:, C_ROWW:C_ROWW + HC] = row * a / (H * W)
    return c


def build(nc, x, w_down, w_conv, w_up, w_guide, w_fuse, bn, consts, out):
    with ExitStack() as ctx:
        def sb(name, shape, dt=F32):
            return ctx.enter_context(nc.sbuf_tensor(name, shape, dt))

        def sem(name):
            return ctx.enter_context(nc.semaphore(name))

        conv = sb("conv", [P, 2, TILES * PX + WC])
        xin = sb("xin", [P, 2, 2, XR + 1, W])
        xres = sb("xres", [P, 2, 2, XR, W])
        interp = sb("interp", [P, XR, W])
        pairs = sb("pairs", [P, CR + 1, P])
        stage = sb("stage", [P, CR + 2, WC])
        taps = sb("taps", [P, TILES, len(PE_TAPS), P])
        junk = sb("junk", [P, XR * W], BF16)
        cst = sb("cst", [P, C_ALL])
        ones = sb("ones", [P, P])
        wd = sb("wd", [P, TILES, 18])
        wc = sb("wc", [P, K, N])
        wu = sb("wu", [P, TILES, 2])
        wg = sb("wg", [P, TILES * 2, P])
        wf = sb("wf", [P, TILES * 2, P])
        bnp = sb("bnp", [P, 4, TILES * 2])
        inv_std = sb("inv_std", [P, TILES * 2])
        lo = sb("lo", [P, TILES])
        hi = sb("hi", [P, TILES])
        xnorm = sb("xnorm", [P, 2, TILES, P])
        xnormT = sb("xnormT", [P, 2, TILES * P])
        gram = sb("gram", [P, TILES, TILES * P])
        gdiag = sb("gdiag", [P, P])
        sq = sb("sq", [P, TILES])
        cent = sb("cent", [P, TILES, K])
        dots = sb("dots", [P, TILES, K])
        dist = sb("dist", [P, TILES, K])
        kt = sb("kt", [P, TILES, K])
        kbest = sb("kbest", [P, TILES])
        member = sb("member", [P, TILES, K])
        member_n = sb("member_n", [P, TILES, K])
        cnt = sb("cnt", [P, 3, K])
        kstat = sb("kstat", [K, PX // BLK, 6])
        kmv = sb("kmv", [K, 2])
        kvd = sb("kvd", [K, K])
        kv = sb("kv", [P, K])
        klt = sb("klt", [P, K, K])
        keq = sb("keq", [P, K, K])
        rank = sb("rank", [P, K])
        sorted_member = sb("sorted_member", [P, TILES, K])
        mean_w = sb("mean_w", [P, TILES, K])
        meansT = sb("meansT", [K, BLK])
        data = sb("data", [P, CHUNKS, K])
        ta = sb("ta", [P, N, CHUNKS * K])
        tb = sb("tb", [P, N, CHUNKS * K])
        mu = sb("mu", [P, N, K])
        varw = sb("varw", [P, N, K + 1])
        logs = sb("logs", [P, N, K + 1])
        ivar = sb("ivar", [P, N, K])
        lconst = sb("lconst", [P, N])
        logp = sb("logp", [P, N, CHUNKS])
        lmax = sb("lmax", [P, CHUNKS])
        esum = sb("esum", [P, CHUNKS])
        resp = sb("resp", [P, N, CHUNKS])
        part = sb("part", [P, N, 2 * K + 1])
        rn = sb("rn", [P, N])
        small = sb("small", [P, 8, K])
        xsum = sb("xsum", [P, 2, TILES, 2, S])
        csum = sb("csum", [P, TILES, HC])
        cedge = sb("cedge", [P, TILES, HC])
        cmean = sb("cmean", [P, TILES])
        gate = sb("gate", [P, TILES])
        gt = sb("gt", [P, TILES, K])
        nscale = sb("nscale", [P, TILES, 2])
        chmean = sb("chmean", [P, TILES, 2])
        squeeze = sb("squeeze", [P, 1])
        scale = sb("scale", [P, TILES * 2])
        shift = sb("shift", [P, TILES * 2])
        ps = ctx.enter_context(nc.psum_tensor("ps", [P, 8, 512], F32))

        ident = cst[:, C_ID:C_ID + P]

        passed = sem("passed")
        setup_in = sem("setup_in")
        taps_ready = sem("taps_ready")
        bn_var = sem("bn_var")
        bn_root = sem("bn_root")
        x_in = [sem(f"x_in{h}") for h in range(2)]
        xres_in = [sem(f"xres_in{h}") for h in range(2)]
        stored = [sem(f"stored{h}") for h in range(2)]
        halo = sem("halo")
        conv_ps = sem("conv_ps")
        conv_taken = sem("conv_taken")
        conv_done = sem("conv_done")
        xsummed = sem("xsummed")
        staged = sem("staged")
        tp = [sem(f"tp{i}") for i in range(3)]
        tc = [sem(f"tc{i}") for i in range(3)]
        interp_ready = sem("interp_ready")
        up_ps = [sem(f"up_ps{i}") for i in range(2)]
        up_taken = [sem(f"up_taken{i}") for i in range(2)]
        shifted = sem("shifted")
        result = sem("result")
        km_x = sem("km_x")
        km_t = [sem(f"km_t{h}") for h in range(2)]
        km_c = [sem(f"km_c{h}") for h in range(2)]
        km_g = sem("km_g")
        km_dve = sem("km_dve")
        km_pe = sem("km_pe")
        km_done = sem("km_done")
        v_ps = [sem(f"v_ps{h}") for h in range(2)]
        v_sb = sem("v_sb")
        v_tp = sem("v_tp")
        v_data = sem("v_data")
        em_stat = sem("em_stat")
        em_stat_ps = sem("em_stat_ps")
        em_var = sem("em_var")
        em_logs = sem("em_logs")
        em_logp = sem("em_logp")
        em_exp = sem("em_exp")
        em_part = sem("em_part")
        em_sum = sem("em_sum")
        fin_dve = sem("fin_dve")
        fin_act = sem("fin_act")
        fin_pe = sem("fin_pe")
        params = sem("params")

        SETUP_DMAS = 7
        xv = x.rearrange("b (t c i) (s r) w -> b t c i s (r w)", t=TILES, i=2, r=XR)
        ov = out.rearrange("b (t c i) (s r) w -> b t c i s (r w)", t=TILES, i=2, r=XR)

        def dram(view, b, t, s):
            return view[ds(b, 1), t, :, :, ds(s, 1), :].rearrange("a c i s f -> c (a i) (s f)")

        def stages(eng, stage_body):
            stage_body(0, 0, True, False, False)
            stage_body(1, 1, True, True, False)
            with eng.Fori(1, B // 2) as jj:
                for p in range(2):
                    stage_body(2 * jj + p, p, True, True, True)
            stage_body(B, 0, False, True, True)
            stage_body(B + 1, 1, False, False, True)

        def runs(eng, em, body, first):
            if not em:
                for t in range(TILES):
                    with eng.Fori(0, U) as u:
                        body(t, u, None)
                return
            body(0, 0, None)
            with eng.Fori(1, U) as u:
                body(0, u, 2 * u - 2)
            with eng.Fori(0, 2) as u:
                body(1, u, 2 * u + 2 * (U - 1))
            first()
            with eng.Fori(2, U) as u:
                body(1, u, None)

        free_from_start = {"tensor": [*tp, *up_ps, v_tp], "scalar": tc,
                           "vector": [conv_taken, *up_taken, v_data]}

        def nothing():
            pass

        def wait_all(eng, *waits):
            waits = [(s_, v if isinstance(v, int) else eng.snap(v)) for s_, v in waits]
            for s_, v in waits:
                eng.wait_ge(s_, v)
            eng.sem_inc(passed)

        block = ctx.enter_context(nc.Block())

        @block.sync
        def _(sp):
            sp.dma_start(cst[:, :], consts).then_inc(setup_in, 16)
            sp.dma_start(wd[:, :, :], w_down).then_inc(setup_in, 16)

            def load(b, t, s, h):
                sp.dma_start(xin[:, h, :, 1:XR + 1, :].rearrange("c i r w -> c i (r w)"),
                             dram(xv, b, t, s)).then_inc(x_in[h], 16)

            def load_again(b, t, s, h):
                sp.dma_start(xres[:, h, :, :, :].rearrange("c i r w -> c i (r w)"),
                             dram(xv, b, t, s)).then_inc(xres_in[h], 16)

            load(0, 0, 0, 0)
            load(0, 0, 1, 1)
            for tile, src in ((wc[:, :, :].rearrange("c k n -> c (k n)"), w_conv), (wu[:, :, :], w_up),
                              (wg[:, :, :], w_guide), (wf[:, :, :], w_fuse), (bnp[:, :, :], bn)):
                sp.dma_start(tile, src).then_inc(setup_in, 16)

            def stage_body(j, do_conv, do_out, more_conv=True, more_out=True):
                def step(t, u, h, nb, nt, nu):
                    g = STEPS * j + S * t + 2 * u + h
                    o = g - 2 * STEPS
                    if do_conv and (nb == 0 or more_conv):
                        wait_all(sp,
                                 (conv_ps, g + 1),
                                 (xsummed, g + 1),
                                 (conv_done, g + 1))
                        wait_all(sp, (halo, g + 2))
                        load(j + nb, nt, 2 * nu + h, h)
                    if do_out:
                        sp.wait_ge(result, o + 1)
                        sp.dma_start(dram(ov, j - 2, t, 2 * u + h),
                                     xres[:, h, :, :, :].rearrange("c i r w -> c i (r w)")) \
                            .then_inc(stored[h], 16)
                        if nb == 0 or more_out:
                            wait_all(sp, (stored[h], 16 * (STEPS // 2 * (j - 2) + U * t + u + 1)))
                            load_again(j - 2 + nb, nt, 2 * nu + h, h)

                for t in range(TILES):
                    with sp.Fori(0, U - 1) as u:
                        for h in range(2):
                            step(t, u, h, 0, t, u + 1)
                    for h in range(2):
                        step(t, U - 1, h, *((0, t + 1, 0) if t + 1 < TILES else (1, 0, 0)))

            stage_body(0, True, False)
            stage_body(1, True, False)
            sp.wait_ge(km_done, 1)
            for h in range(2):
                load_again(0, 0, h, h)
            with sp.Fori(1, B // 2 - 1) as jj:
                for p in range(2):
                    stage_body(2 * jj + p, True, True)
            stage_body(B - 2, True, True)
            stage_body(B - 1, True, True, more_conv=False)
            stage_body(B, False, True)
            stage_body(B + 1, False, True, more_out=False)
            for h in range(2):
                sp.wait_ge(stored[h], 16 * B * STEPS // 2)

        @block.gpsimd
        def _(pool):
            pool.memset(ones[:, :], 1.0)
            pool.memset(stage[:, CR, :], 0.0)
            for p in range(2):
                pool.memset(conv[:, p, TILES * PX:], 0.0)
            pool.wait_ge(setup_in, 16 * SETUP_DMAS)
            for t in range(TILES):
                for n, (i, ky, kx) in enumerate(PE_TAPS):
                    k = 9 * i + 3 * ky + kx
                    pool.tensor_scalar(taps[:, t, n, :], ident, wd[:, t, k:k + 1], None, ALU.mult)
            pool.drain().then_inc(taps_ready, 1)

            def halo_row(g, h, prev_count):
                wait_all(pool,
                         (conv_done, g - 1),
                         (x_in[1 - h], prev_count))
                pool.tensor_copy(xin[:, h, :, 0, :], xin[:, 1 - h, :, XR, :]).then_inc(halo, 1)

            def halo_zero(g):
                if not (isinstance(g, int) and g == 0):
                    wait_all(pool,
                             (conv_done, g - 1))
                pool.memset(xin[:, 0, :, 0, :], 0.0).then_inc(halo, 1)

            def stage_body(j, p, do_conv, do_em, do_out):
                def halos(t, u, top):
                    g = STEPS * j + S * t + 2 * u
                    landed = 8 * (STEPS * j + S * t) + 16 * u
                    if top:
                        halo_zero(g)
                    else:
                        halo_row(g, 0, landed)
                    halo_row(g + 1, 1, landed + 16)

                def rows(t, u, h):
                    o = STEPS * (j - 2) + S * t + 2 * u + h
                    wait_all(pool,
                             (tp[2], o + 1))
                    pool.tensor_copy(stage[:, 0, :], stage[:, CR, :])
                    pool.drain()
                    pool.tensor_copy(stage[:, 1:, :],
                                     conv[:, p, ds(t * PX + CN * (2 * u + h), CN + WC)]
                                     .rearrange("c (r w) -> c r w", w=WC)).then_inc(staged, 1)

                def weights(t, u, h):
                    o = STEPS * (j - 2) + S * t + 2 * u + h
                    pool.wait_ge(up_ps[1], o + 1)
                    pool.tensor_tensor(
                        interp[:, :, :],
                        cst[:, ds(C_COEF + XR * (2 * u + h), XR)].unsqueeze(2).to_broadcast([P, XR, W]),
                        cst[:, C_U:C_U + W].unsqueeze(1).to_broadcast([P, XR, W]),
                        ALU.mult).then_inc(interp_ready, 1)

                def round_(t, u, top):
                    if not do_out:
                        halos(t, u, top)
                        return
                    rows(t, u, 0)
                    if do_conv:
                        g = STEPS * j + S * t + 2 * u
                        landed = 8 * (STEPS * j + S * t) + 16 * u
                        if top:
                            halo_zero(g)
                        else:
                            halo_row(g, 0, landed)
                    weights(t, u, 0)
                    rows(t, u, 1)
                    if do_conv:
                        halo_row(g + 1, 1, landed + 16)
                    weights(t, u, 1)

                if do_out:
                    pool.wait_ge(conv_done, STEPS * (j - 1))
                for t in range(TILES):
                    round_(t, 0, True)
                    with pool.Fori(1, U) as u:
                        round_(t, u, False)

            stage_body(0, 0, True, False, False)
            stage_body(1, 1, True, True, False)
            pool.wait_ge(km_done, 1)
            with pool.Fori(1, B // 2) as jj:
                for p in range(2):
                    stage_body(2 * jj + p, p, True, True, True)
            stage_body(B, 0, False, True, True)
            stage_body(B + 1, 1, False, False, True)

        @block.scalar
        def _(act):
            for free in free_from_start["scalar"]:
                act.sem_inc(free)
            act.wait_ge(bn_var, 1)
            act.activation(inv_std[:, :], inv_std[:, :], ACT.Sqrt).then_inc(bn_root, 1)
            act.preload_act_table_set("natural_log_exp_and_others")

            def k_means():
                def copy_round(q):
                    for h in range(2):
                        act.wait_ge(km_t[h], q + 1)
                        if not (isinstance(q, int) and q == 0):
                            act.wait_ge(km_g, q)
                        act.activation(xnormT[:, h, :], ps[:, PS_T + h, 0:TILES * P], ACT.Copy) \
                            .then_inc(km_c[h], 1)
                copy_round(0)
                with act.Fori(1, CHUNKS // 2) as q:
                    copy_round(q)

            def means(b):
                with act.Fori(0, PX // BLK // 2) as v:
                    for h in range(2):
                        n = PX // BLK * b + 2 * v + h
                        act.wait_ge(v_ps[h], PX // BLK // 2 * b + v + 1)
                        act.wait_ge(v_tp, n + 1)
                        act.activation(meansT[:, :], ps[0:K, PS_T + h, :], ACT.Copy).then_inc(v_sb, 1)

            def stage_body(j, p, do_conv, do_em, do_out):
                def step(t, u, h, em):
                    g = STEPS * j + S * t + 2 * u + h
                    o = g - 2 * STEPS
                    if do_out:
                        act.wait_ge(up_ps[1], o + 1)
                        act.wait_ge(tp[0], o + 2)
                        act.activation(pairs[:, CR, :], ps[:, PS_CONV, 0:P], ACT.Copy).then_inc(tc[0], 1)
                        for i in range(2):
                            act.wait_ge(tp[1 + i], o + 2)
                            act.activation(pairs[:, 4 * i:4 * i + 4, :].rearrange("c r w -> c (r w)"),
                                           ps[:, PS_T + i, :], ACT.Copy).then_inc(tc[1 + i], 1)
                    if em is not None:
                        e = EM_ITERS * (j - 1) + em + h
                        act.wait_ge(em_var, (EM_ITERS + 1) * (j - 1) + em + h + 1)
                        act.activation(logs[:, :, :], varw[:, :, :], ACT.Ln).then_inc(em_logs, 1)
                        act.wait_ge(em_logp, e + 1)
                        act.activation(resp[:, :, :], logp[:, :, :], ACT.Exp).then_inc(em_exp, 1)
                    if do_out:
                        act.wait_ge(xres_in[h], 8 * (STEPS * (j - 2) + S * t) + 16 * u + 16)
                        for i in range(2):
                            c = xres[:, h, i, :, :].rearrange("c r w -> c (r w)")
                            y = act.activation(c, c, ACT.Identity, bias=shift[:, 2 * t + i:2 * t + i + 1])
                        y.then_inc(shifted, 1)
                    if do_conv:
                        act.wait_ge(x_in[h], 8 * (STEPS * j + S * t) + 16 * u + 16)
                        for i in range(2):
                            act.activation(junk[:, :], xin[:, h, i, 1:, :].rearrange("c r w -> c (r w)"),
                                           ACT.Copy, accum_out=xsum[:, p, t, i, ds(2 * u + h, 1)])
                            d = act.drain()
                        d.then_inc(xsummed, 1)

                def round_(t, u, em):
                    for h in range(2):
                        step(t, u, h, em)

                if do_out:
                    act.wait_ge(params, j - 1)
                if do_em:
                    means(j - 1)
                runs(act, do_em, round_, nothing)
                if do_em:
                    act.wait_ge(fin_dve, 3 * (j - 1) + 1)
                    act.activation(small[:, 3, :], small[:, 2, :], ACT.Exp, scale=-1.0).then_inc(fin_act, 1)

            stage_body(0, 0, True, False, False)
            k_means()
            stage_body(1, 1, True, True, False)
            with act.Fori(1, B // 2) as jj:
                for p in range(2):
                    stage_body(2 * jj + p, p, True, True, True)
            stage_body(B, 0, False, True, True)
            stage_body(B + 1, 1, False, False, True)

        @block.tensor
        def _(pe):
            for free in free_from_start["tensor"]:
                pe.sem_inc(free)
            pe.wait_ge(taps_ready, 1)

            def k_means():
                def gram_round(q, first, last):
                    for h in range(2):
                        pe.wait_ge(km_x, 2 * q + h + 1)
                        if not first:
                            pe.wait_ge(km_c[h], q)
                        for t in range(TILES):
                            m = pe.transpose(ps[:, PS_T + h, t * P:(t + 1) * P], xnorm[:, h, t, :], ident)
                        m.then_inc(km_t[h], 1)
                    for h in range(2):
                        pe.wait_ge(km_c[h], q + 1)
                        for a in range(TILES):
                            m = pe.matmul(ps[:, PS_UP + a, 0:TILES * P], xnormT[:, h, a * P:(a + 1) * P],
                                          xnormT[:, h, :], start=first and h == 0, stop=last and h == 1)
                    m.then_inc(km_g, 1)
                gram_round(0, True, False)
                with pe.Fori(1, CHUNKS // 2 - 1) as q:
                    gram_round(q, False, False)
                gram_round(CHUNKS // 2 - 1, False, True)

                def over_channels(col, weights, values, n):
                    pe.wait_ge(km_dve, n + 1)
                    for t in range(TILES):
                        m = pe.matmul(ps[:, PS_SMALL, col:col + K], weights(t), values[:, t, :],
                                      start=t == 0, stop=t == TILES - 1)
                    return m

                with pe.Fori(0, KM_ITERS + 1) as it:
                    for a in range(TILES):
                        m = over_channels(K * a, lambda t: gram[:, t, a * P:(a + 1) * P], cent, 3 * it)
                    m.then_inc(km_pe, 1)
                    over_channels(2 * K, lambda t: ones[:, :], kt, 3 * it + 1).then_inc(km_pe, 1)
                    over_channels(3 * K, lambda t: ones[:, :], member, 3 * it + 2).then_inc(km_pe, 1)
                n = 3 * (KM_ITERS + 1)
                pe.wait_ge(km_dve, n + 1)
                for c in range(PX // BLK):
                    if c >= 2:
                        pe.wait_ge(km_dve, n + c)
                    for t in range(TILES):
                        m = pe.matmul(ps[0:K, PS_T + c % 2, :], member_n[:, t, :],
                                      conv[:, 0, t * PX + BLK * c:t * PX + BLK * (c + 1)],
                                      start=t == 0, stop=t == TILES - 1)
                    m.then_inc(km_pe, 1)
                n += PX // BLK + 2
                pe.wait_ge(km_dve, n)
                pe.matmul(ps[:, PS_SMALL, 4 * K:5 * K], ones[0:K, :], kvd[:, :], start=True, stop=True) \
                    .then_inc(km_pe, 1)
                pe.wait_ge(km_done, 1)

            def means(b, p):
                with pe.Fori(0, PX // BLK // 2) as v:
                    for h in range(2):
                        n = PX // BLK * b + 2 * v + h
                        for t in range(TILES):
                            m = pe.matmul(ps[0:K, PS_T + h, :], mean_w[:, t, :],
                                          conv[:, p, ds(t * PX + BLK * (2 * v + h), BLK)],
                                          start=t == 0, stop=t == TILES - 1)
                        m.then_inc(v_ps[h], 1)
                        pe.wait_ge(v_sb, n + 1)
                        pe.wait_ge(v_data, n + 1)
                        for c in range(BLK // P):
                            m = pe.matmul(ps[:, PS_SMALL, c * K:(c + 1) * K],
                                          meansT[:, c * P:(c + 1) * P], ident[0:K, 0:K],
                                          start=True, stop=True)
                        m.then_inc(v_tp, 1)
                for n in range(3):
                    pe.wait_ge(em_stat, 3 * b + n + 1)
                    if n == 0:
                        pe.matmul(ps[:, PS_SMALL, SM_SUM:SM_SUM + K], cst[:, C_FIRST:C_FIRST + P],
                                  data[:, 0, :], start=True, stop=True)
                        m = pe.matmul(ps[:, PS_SMALL, SM_SUM + K:SM_SUM + 2 * K],
                                      cst[:, C_LAST:C_LAST + P], data[:, CHUNKS - 1, :],
                                      start=True, stop=True)
                    else:
                        m = pe.matmul(ps[:, PS_SMALL, SM_SUM:SM_SUM + K], ones[:, :], part[:, 0, 0:K],
                                      start=True, stop=True)
                    m.then_inc(em_stat_ps, 1)

            def stage_body(j, p, do_conv, do_em, do_out):
                def step(t, u, h, em):
                    g = STEPS * j + S * t + 2 * u + h
                    o = g - 2 * STEPS
                    if do_out:
                        pe.wait_ge(staged, o + 1)
                        pe.wait_ge(conv_taken, g + 1 if do_conv else B * STEPS + 1)
                        pe.transpose(ps[:, PS_CONV, 0:P],
                                     stage[:, CR:CR + 2, :].rearrange("c r w -> c (r w)"), ident) \
                            .then_inc(tp[0], 1)
                        for i in range(2):
                            pe.wait_ge(tc[1 + i], o + 1)
                            for m in range(4):
                                k = 4 * i + m
                                mm = pe.transpose(ps[:, PS_T + i, m * P:(m + 1) * P],
                                                  stage[:, k:k + 2, :].rearrange("c r w -> c (r w)"), ident)
                            mm.then_inc(tp[1 + i], 1)
                    if do_conv:
                        pe.wait_ge(x_in[h], 8 * (STEPS * j + S * t) + 16 * u + 16)
                        pe.wait_ge(conv_taken, g + 1)
                        if do_out:
                            pe.wait_ge(tc[0], o + 2)
                        acc = ps[:, PS_CONV, :].rearrange("c (r w) -> c r w", w=WC)
                        for n, (i, ky, kx) in enumerate(PE_TAPS):
                            rows = slice(ky, ky + XR - 1, 2)
                            last = n == len(PE_TAPS) - 1
                            if kx == 0:
                                mm = pe.matmul(acc[:, :, 1:], taps[:, t, n, :],
                                               xin[:, h, i, rows, 1:W - 2:2], start=n == 0, stop=last)
                            else:
                                mm = pe.matmul(acc, taps[:, t, n, :],
                                               xin[:, h, i, rows, kx - 1:W:2], start=n == 0, stop=last)
                        mm.then_inc(conv_ps, 1)
                    if em is not None:
                        e = EM_ITERS * (j - 1) + em + h
                        pe.wait_ge(em_part, e + 1)
                        pe.matmul(ps[:, PS_SMALL, SM_SUM:SM_SUM + N * (2 * K + 1)], ones[:, :],
                                  part[:, :, :].rearrange("c n k -> c (n k)"),
                                  start=True, stop=True).then_inc(em_sum, 1)
                    if do_out:
                        pe.wait_ge(interp_ready, o + 1)
                        for i in range(3):
                            pe.wait_ge(tc[i], o + 2)
                        for half, ms in ((0, (1, 2, 3, 4)), (1, (5, 6, 7, 8, 0))):
                            pe.wait_ge(up_taken[half], o + 1)
                            for m in ms:
                                pos, n = (2 * m - 2, 2) if 0 < m < CR else (2 * CR - 2, 1) if m else (2 * CR - 1, 1)
                                mm = pe.matmul(ps[:, PS_UP + pos // 4, (pos % 4) * W:(pos % 4 + n) * W],
                                               pairs[:, m, :],
                                               interp[:, pos:pos + n, :].rearrange("c r w -> c (r w)"),
                                               start=True, stop=True)
                            mm.then_inc(up_ps[half], 1)

                def round_(t, u, em):
                    for h in range(2):
                        step(t, u, h, em)

                if do_em:
                    if do_out:
                        for i in range(2):
                            wait_all(pe, (tc[1 + i], STEPS * (j - 2) + 1))
                    means(j - 1, 1 - p)
                runs(pe, do_em, round_, nothing)
                if do_em:
                    pe.wait_ge(fin_dve, 3 * (j - 1) + 2)
                    for n in range(2 * TILES):
                        m = pe.matmul(ps[:, PS_SMALL, SM_Y1:SM_Y1 + 1], wg[:, n, :],
                                      chmean[:, :, :].rearrange("c t i -> c (t i)")[:, n:n + 1],
                                      start=n == 0, stop=n == 2 * TILES - 1)
                    m.then_inc(fin_pe, 1)
                    pe.wait_ge(fin_dve, 3 * (j - 1) + 3)
                    for n in range(2 * TILES):
                        m = pe.matmul(ps[:, PS_SMALL, SM_Y2 + n:SM_Y2 + n + 1], wf[:, n, :],
                                      squeeze[:, :], start=True, stop=True)
                    m.then_inc(fin_pe, 1)

            stage_body(0, 0, True, False, False)
            k_means()
            stage_body(1, 1, True, True, False)
            with pe.Fori(1, B // 2) as jj:
                for p in range(2):
                    stage_body(2 * jj + p, p, True, True, True)
            stage_body(B, 0, False, True, True)
            stage_body(B + 1, 1, False, False, True)

        @block.vector
        def _(dve):
            def tt(out_, a, b, op):
                dve.tensor_tensor(out_, a, b, op)
                return dve.drain()

            def tsc(out_, a, s1, s2, op0, op1=ALU.bypass):
                dve.tensor_scalar(out_, a, s1, s2, op0, op1) if s2 is not None else \
                    dve.tensor_scalar(out_, a, s1, None, op0)
                return dve.drain()

            def stt(out_, a, s, b, op0, op1):
                dve.scalar_tensor_tensor(out_, a, s, b, op0, op1)
                return dve.drain()

            def red(out_, a, op=ALU.add):
                dve.tensor_reduce(out_, a, AX.X, op)
                return dve.drain()

            def recip(out_, a):
                dve.reciprocal(out_, a)
                return dve.drain()

            for free in free_from_start["vector"]:
                dve.sem_inc(free)
            dve.wait_ge(setup_in, 16 * SETUP_DMAS)
            tsc(inv_std[:, :], bnp[:, 3, :], BN_EPS, None, ALU.add).then_inc(bn_var, 1)
            dve.wait_ge(bn_root, 1)
            recip(inv_std[:, :], inv_std[:, :])

            def k_means():
                both = conv[:, 0, 0:TILES * PX].rearrange("c (t x) -> c t x", t=TILES)
                dve.tensor_reduce(lo[:, :], both, AX.X, ALU.min)
                red(hi[:, :], both, ALU.max)
                tt(hi[:, :], hi[:, :], lo[:, :], ALU.subtract)
                tsc(hi[:, :], hi[:, :], 1e-12, None, ALU.max)
                recip(hi[:, :], hi[:, :])

                def normalise(q):
                    for h in range(2):
                        if not (isinstance(q, int) and q == 0):
                            dve.wait_ge(km_t[h], q)
                        for t in range(TILES):
                            m = dve.tensor_scalar(xnorm[:, h, t, :],
                                                  conv[:, 0, ds(t * PX + P * (2 * q + h), P)],
                                                  lo[:, t:t + 1], hi[:, t:t + 1], ALU.subtract, ALU.mult)
                        m.then_inc(km_x, 1)
                normalise(0)
                with dve.Fori(1, CHUNKS // 2) as q:
                    normalise(q)

                dve.wait_ge(km_g, CHUNKS // 2)
                for a in range(TILES):
                    dve.tensor_copy(gram[:, a, :], ps[:, PS_UP + a, 0:TILES * P])
                dve.drain()
                for a in range(TILES):
                    tt(gdiag[:, :], gram[:, a, a * P:(a + 1) * P], ident, ALU.mult)
                    red(sq[:, a:a + 1], gdiag[:, :])
                dve.tensor_copy(cent[:, :, :].rearrange("c t k -> c (t k)"),
                                cst[:, C_SEED:C_SEED + TILES * K]).then_inc(km_dve, 1)

                def wide(v, shape=(P, TILES, K)):
                    return v.unsqueeze(1 if v.shape[1] == K else 2).to_broadcast(list(shape))

                prefer = cst[:, C_PREF:C_PREF + K]
                with dve.Fori(0, KM_ITERS + 1) as it:
                    dve.wait_ge(km_pe, 3 * it + 1)
                    dve.tensor_copy(dots[:, :, :].rearrange("c t k -> c (t k)"),
                                    ps[:, PS_SMALL, 0:TILES * K])
                    dve.drain()
                    tt(kt[:, :, :], dots[:, :, :], cent[:, :, :], ALU.mult).then_inc(km_dve, 1)
                    dve.wait_ge(km_pe, 3 * it + 2)
                    tt(dist[:, :, :], wide(ps[:, PS_SMALL, 2 * K:3 * K]), wide(sq[:, :]), ALU.add)
                    stt(dist[:, :, :].rearrange("c t k -> c (t k)"),
                        dots[:, :, :].rearrange("c t k -> c (t k)"), -2.0,
                        dist[:, :, :].rearrange("c t k -> c (t k)"), ALU.mult, ALU.add)
                    red(kbest[:, :], dist[:, :, :], ALU.min)
                    tt(dist[:, :, :], dist[:, :, :], wide(kbest[:, :]), ALU.is_equal)
                    tt(dist[:, :, :], dist[:, :, :], wide(prefer), ALU.mult)
                    red(kbest[:, :], dist[:, :, :], ALU.max)
                    tt(member[:, :, :], dist[:, :, :], wide(kbest[:, :]), ALU.is_equal) \
                        .then_inc(km_dve, 1)
                    dve.wait_ge(km_pe, 3 * it + 3)
                    tsc(cnt[:, 0, :], ps[:, PS_SMALL, 3 * K:4 * K], 1.0, None, ALU.max)
                    tsc(cnt[:, 2, :], ps[:, PS_SMALL, 3 * K:4 * K], 0.0, None, ALU.is_le)
                    recip(cnt[:, 1, :], cnt[:, 0, :])
                    tt(cent[:, :, :], cent[:, :, :], wide(cnt[:, 2, :]), ALU.mult)
                    tt(member_n[:, :, :], member[:, :, :], wide(cnt[:, 1, :]), ALU.mult)
                    tt(cent[:, :, :], cent[:, :, :], member_n[:, :, :], ALU.add).then_inc(km_dve, 1)
                for c in range(PX // BLK):
                    dve.wait_ge(km_pe, 3 * (KM_ITERS + 1) + c + 1)
                    dve.bn_stats(kstat[:, c, :], ps[0:K, PS_T + c % 2, :])
                    dve.drain().then_inc(km_dve, 1)
                dve.bn_aggr(kmv[:, :], kstat[:, :, :].rearrange("k c s -> k (c s)"))
                dve.drain()
                tsc(kvd[:, :], ident[0:K, 0:K], kmv[:, 1:2], None, ALU.mult).then_inc(km_dve, 1)
                dve.wait_ge(km_pe, 3 * (KM_ITERS + 1) + PX // BLK + 1)
                dve.tensor_copy(kv[:, :], ps[:, PS_SMALL, 4 * K:5 * K])
                dve.drain()
                other = kv[:, :].unsqueeze(1).to_broadcast([P, K, K])
                own = kv[:, :].unsqueeze(2).to_broadcast([P, K, K])
                tt(klt[:, :, :], other, own, ALU.is_lt)
                tt(keq[:, :, :], other, own, ALU.is_equal)
                tt(keq[:, :, :], keq[:, :, :], cst[:, C_TRI:C_TRI + K * K].rearrange("c (k m) -> c k m", k=K),
                   ALU.mult)
                tt(klt[:, :, :], klt[:, :, :], keq[:, :, :], ALU.add)
                red(rank[:, :], klt[:, :, :])
                tt(kt[:, :, :], member[:, :, :], wide(rank[:, :]), ALU.mult)
                red(kbest[:, :], kt[:, :, :])
                tt(sorted_member[:, :, :], wide(kbest[:, :]), wide(cst[:, C_IOTA:C_IOTA + K]), ALU.is_equal)
                red(kbest[:, :], member_n[:, :, :])
                tt(mean_w[:, :, :], sorted_member[:, :, :], wide(kbest[:, :]), ALU.mult).then_inc(km_done, 1)

            d_ck = data[:, :, :]
            d_kc = data[:, :, :].rearrange("p c k -> p k c")
            flat = data[:, :, :].rearrange("p c k -> p (c k)")

            def mix_view(t_, order):
                return t_[:, :, :].rearrange("p n (a b) -> p n a b", a=CHUNKS if order == "ck" else K)

            def per_k(v):
                return v.unsqueeze(2).to_broadcast([P, N, CHUNKS, K])

            def means(b):
                with dve.Fori(0, PX // BLK) as v:
                    dve.wait_ge(v_tp, PX // BLK * b + v + 2)
                    dve.tensor_copy(data[:, ds(v * (BLK // P), BLK // P), :].rearrange("p c k -> p (c k)"),
                                    ps[:, PS_SMALL, 0:BLK // P * K]).then_inc(v_data, 1)
                dve.drain().then_inc(em_stat, 1)
                red(part[:, 0, 0:K], d_kc)
                dve.wait_ge(em_stat_ps, 3 * b + 1)
                dve.tensor_copy(mu[:, :, :].rearrange("p n k -> p (n k)"),
                                ps[:, PS_SMALL, SM_SUM:SM_SUM + N * K])
                dve.drain().then_inc(em_stat, 1)
                dve.wait_ge(em_stat_ps, 3 * b + 2)
                tsc(small[:, 0, :], ps[:, PS_SMALL, SM_SUM:SM_SUM + K], 1.0 / PX, None, ALU.mult)
                dev = mix_view(ta, "ck")[:, 0, :, :]
                tt(dev, d_ck, small[:, 0, :].unsqueeze(1).to_broadcast([P, CHUNKS, K]), ALU.subtract)
                tt(dev, dev, dev, ALU.mult)
                red(part[:, 0, 0:K], dev.rearrange("p c k -> p k c")).then_inc(em_stat, 1)
                dve.wait_ge(em_stat_ps, 3 * b + 3)
                for n in range(N):
                    dve.tensor_scalar(varw[:, n, 0:K], ps[:, PS_SMALL, SM_SUM:SM_SUM + K], 1.0 / PX, EPS,
                                      ALU.mult, ALU.add)
                    dve.memset(varw[:, n, K:K + 1], 1.0 / N)
                dve.drain().then_inc(em_var, 1)

            def em_expect(e):
                dve.reciprocal(ivar[:, :, :], varw[:, :, 0:K])
                a, b_ = mix_view(ta, "ck"), mix_view(tb, "ck")
                for n in range(N):
                    dve.tensor_tensor(a[:, n, :, :], d_ck,
                                      mu[:, n, :].unsqueeze(1).to_broadcast([P, CHUNKS, K]), ALU.subtract)
                dve.drain()
                tt(tb[:, :, :], ta[:, :, :], ta[:, :, :], ALU.mult)
                for n in range(N):
                    dve.tensor_tensor(a[:, n, :, :], b_[:, n, :, :],
                                      ivar[:, n, :].unsqueeze(1).to_broadcast([P, CHUNKS, K]), ALU.mult)
                dve.drain()
                red(logp[:, :, :], a)
                dve.wait_ge(em_logs, e + 1)
                red(lconst[:, :], logs[:, :, 0:K])
                tsc(lconst[:, :], lconst[:, :], float(K * np.log(2 * np.pi)), -0.5, ALU.add, ALU.mult)
                tt(lconst[:, :], lconst[:, :], logs[:, :, K], ALU.add)
                for n in range(N):
                    dve.tensor_scalar(logp[:, n, :], logp[:, n, :], -0.5, lconst[:, n:n + 1],
                                      ALU.mult, ALU.add)
                dve.drain()
                tt(lmax[:, :], logp[:, 0, :], logp[:, 1, :], ALU.max)
                tt(logp[:, :, :], logp[:, :, :], lmax[:, :].unsqueeze(1).to_broadcast([P, N, CHUNKS]),
                   ALU.subtract).then_inc(em_logp, 1)

            def em_sums(e):
                dve.wait_ge(em_exp, e + 1)
                tt(esum[:, :], resp[:, 0, :], resp[:, 1, :], ALU.add)
                recip(esum[:, :], esum[:, :])
                tt(resp[:, :, :], resp[:, :, :], esum[:, :].unsqueeze(1).to_broadcast([P, N, CHUNKS]),
                   ALU.mult)
                a, b_ = mix_view(ta, "kc"), mix_view(tb, "kc")
                for n in range(N):
                    dve.tensor_tensor(a[:, n, :, :], d_kc,
                                      resp[:, n, :].unsqueeze(1).to_broadcast([P, K, CHUNKS]), ALU.mult)
                dve.tensor_reduce(part[:, :, 2 * K], resp[:, :, :], AX.X, ALU.add)
                dve.drain()
                for n in range(N):
                    dve.tensor_tensor(b_[:, n, :, :], d_kc, a[:, n, :, :], ALU.mult)
                dve.tensor_reduce(part[:, :, 0:K], a, AX.X, ALU.add)
                dve.drain()
                red(part[:, :, K:2 * K], b_).then_inc(em_part, 1)

            def em_update(e):
                dve.wait_ge(em_sum, e + 1)
                sums = ps[:, PS_SMALL, SM_SUM:SM_SUM + N * (2 * K + 1)].rearrange("p (n k) -> p n k", n=N)
                dve.tensor_scalar(varw[:, :, K], sums[:, :, 2 * K], 1.0 / PX, None, ALU.mult)
                recip(rn[:, :], sums[:, :, 2 * K])
                over = rn[:, :].unsqueeze(2).to_broadcast([P, N, K])
                dve.tensor_tensor(mu[:, :, :], sums[:, :, 0:K], over, ALU.mult)
                tt(varw[:, :, 0:K], sums[:, :, K:2 * K], over, ALU.mult)
                tt(ivar[:, :, :], mu[:, :, :], mu[:, :, :], ALU.mult)
                tt(varw[:, :, 0:K], varw[:, :, 0:K], ivar[:, :, :], ALU.subtract)
                tsc(varw[:, :, 0:K], varw[:, :, 0:K], EPS, EPS, ALU.add, ALU.max).then_inc(em_var, 1)

            def conv_sums(q):
                rows = conv[:, q, 0:TILES * PX].rearrange("c (h w) -> c h w", w=WC)
                sums = csum[:, :, :].rearrange("c t h -> c (t h)")
                edges = cedge[:, :, :].rearrange("c t h -> c (t h)")
                dve.tensor_reduce(sums, rows, AX.X, ALU.add)
                dve.tensor_tensor(edges, rows[:, :, 0], rows[:, :, WC - 1], ALU.add)
                dve.drain()
                stt(sums, edges, -0.25, sums, ALU.mult, ALU.add)
                tt(csum[:, :, :], csum[:, :, :],
                   cst[:, C_ROWW:C_ROWW + HC].unsqueeze(1).to_broadcast([P, TILES, HC]), ALU.mult)
                red(cmean[:, :], csum[:, :, :])

            def finish(b, q):
                le, gt_, z, ez, s0, s1 = (small[:, i, :] for i in (0, 1, 2, 3, 4, 5))
                tt(le, varw[:, 0, 0:K], varw[:, 1, 0:K], ALU.is_le)
                tsc(gt_, le, -1.0, 1.0, ALU.mult, ALU.add)
                for n, first, second in ((0, le, gt_), (1, gt_, le)):
                    tt(s0, first, mu[:, 0, :], ALU.mult)
                    tt(s1, second, mu[:, 1, :], ALU.mult)
                    tt(s0, s0, s1, ALU.add)
                    tt(s0, s0, wc[:, :, n], ALU.mult)
                    if n == 0:
                        dve.tensor_copy(z, s0)
                        dve.drain()
                    else:
                        tt(z, z, s0, ALU.add).then_inc(fin_dve, 1)
                dve.wait_ge(fin_act, b + 1)
                tsc(s0, ez, 1.0, None, ALU.add)
                recip(s0, s0)
                tt(gt[:, :, :], sorted_member[:, :, :], s0.unsqueeze(1).to_broadcast([P, TILES, K]), ALU.mult)
                red(gate[:, :], gt[:, :, :])
                tsc(gate[:, :], gate[:, :], 1.0, None, ALU.add)
                tt(nscale[:, :, :], wu[:, :, :], gate[:, :].unsqueeze(2).to_broadcast([P, TILES, 2]), ALU.mult)
                dve.wait_ge(xsummed, STEPS * (b + 1))
                dve.tensor_reduce(chmean[:, :, :].rearrange("c t i -> c (t i)"),
                                  xsum[:, q, :, :, :].rearrange("c t i s -> c (t i) s"), AX.X, ALU.add)
                tt(gt[:, :, 0:2], nscale[:, :, :], cmean[:, :].unsqueeze(2).to_broadcast([P, TILES, 2]),
                   ALU.mult)
                for t in range(TILES):
                    dve.scalar_tensor_tensor(chmean[:, t, :], chmean[:, t, :], 1.0 / (H * W),
                                             gt[:, t, 0:2], ALU.mult, ALU.add)
                dve.drain().then_inc(fin_dve, 1)
                dve.wait_ge(fin_pe, 2 * b + 1)
                tsc(squeeze[:, :], ps[:, PS_SMALL, SM_Y1:SM_Y1 + 1], 0.0, 6.0, ALU.max, ALU.min) \
                    .then_inc(fin_dve, 1)
                dve.wait_ge(fin_pe, 2 * b + 2)
                y = small[:, 6, 0:2 * TILES]
                tt(y, ps[:, PS_SMALL, SM_Y2:SM_Y2 + 2 * TILES], bnp[:, 2, :], ALU.subtract)
                tt(y, y, inv_std[:, :], ALU.mult)
                tt(y, y, bnp[:, 0, :], ALU.mult)
                tt(y, y, bnp[:, 1, :], ALU.add)
                if not (isinstance(b, int) and b == 0):
                    dve.wait_ge(shifted, STEPS * b)
                dve.tensor_copy(scale[:, :], nscale[:, :, :].rearrange("c t i -> c (t i)"))
                tsc(shift[:, :], y, 0.0, 6.0, ALU.max, ALU.min).then_inc(params, 1)

            def stage_body(j, p, do_conv, do_em, do_out):
                def step(t, u, h, em):
                    g = STEPS * j + S * t + 2 * u + h
                    o = g - 2 * STEPS
                    if em is not None:
                        e = EM_ITERS * (j - 1) + em + h
                        em_expect(e)
                        em_sums(e)
                    if do_conv:
                        dve.wait_ge(x_in[h], 8 * (STEPS * j + S * t) + 16 * u + 16)
                        dve.wait_ge(conv_ps, g + 1)
                        if do_out:
                            dve.wait_ge(staged, o + 1)
                        rows = conv[:, p, ds(t * PX + CN * (2 * u + h), CN)].rearrange(
                            "c (r w) -> c r w", w=WC)
                        acc = ps[:, PS_CONV, :].rearrange("c (r w) -> c r w", w=WC)
                        dve.wait_ge(halo, g + 1)
                        for n, (i, ky, kx) in enumerate(DVE_TAPS):
                            k = 9 * i + 3 * ky + kx
                            last = n == len(DVE_TAPS) - 1
                            src = xin[:, h, i, ky:ky + XR - 1:2, 1:W - 2:2] if kx == 0 else \
                                xin[:, h, i, ky:ky + XR - 1:2, kx - 1:W:2]
                            to, add = (rows[:, :, 1:], rows[:, :, 1:]) if kx == 0 else (rows, rows)
                            if n == 0:
                                add = acc
                            dve.scalar_tensor_tensor(to, src, wd[:, t, k:k + 1], add, ALU.mult, ALU.add)
                            d = dve.drain()
                            if n == 0:
                                d.then_inc(conv_taken, 1)
                            if last:
                                d.then_inc(conv_done, 1)
                    if do_out:
                        dve.wait_ge(shifted, o + 1)
                        for half in range(2):
                            dve.wait_ge(up_ps[half], o + 2)
                            for i in range(2):
                                sc = scale[:, 2 * t + i:2 * t + i + 1]
                                up = ps[:, PS_UP:PS_UP + 4, :].rearrange("c b n -> c (b n)")
                                spans = [(1, 9, 0)] if half == 0 else [(9, XR, CR), (0, 1, XR - 1)]
                                for r0, r1, pos in spans:
                                    dst = xres[:, h, i, r0:r1, :].rearrange("c r w -> c (r w)")
                                    m = dve.scalar_tensor_tensor(dst, up[:, pos * W:(pos + r1 - r0) * W],
                                                                 sc, dst, ALU.mult, ALU.add)
                            m.then_inc(up_taken[half], 1)
                        dve.drain().then_inc(result, 1)
                    if em is not None:
                        em_update(e)

                def round_(t, u, em):
                    for h in range(2):
                        step(t, u, h, em)

                if do_em:
                    means(j - 1)
                runs(dve, do_em, round_, lambda: conv_sums(1 - p))
                if do_em:
                    finish(j - 1, 1 - p)

            stage_body(0, 0, True, False, False)
            k_means()
            stage_body(1, 1, True, True, False)
            with dve.Fori(1, B // 2) as jj:
                for p in range(2):
                    stage_body(2 * jj + p, p, True, True, True)
            stage_body(B, 0, False, True, True)
            stage_body(B + 1, 1, False, False, True)


def kernel(x, L0_conv_w_down, L0_conv_w_conv, L0_conv_w_up, L1_conv_w_guide, L1_conv_w_fuse,
           L1_conv_bn_gamma, L1_conv_bn_beta, L1_conv_bn_mean, L1_conv_bn_var):
    import concourse.bacc as bacc
    from concourse.bass_utils import run_bass_kernel_spmd

    def by_channel(v):
        v = np.asarray(v)
        v = v.reshape(TILES, P, 2, *v.shape[1:])
        return np.ascontiguousarray(np.moveaxis(v, 0, 1).reshape(P, TILES * 2, *v.shape[3:]))

    w_down = np.asarray(L0_conv_w_down).reshape(TILES, P, 18).transpose(1, 0, 2)
    w_conv = np.broadcast_to(np.asarray(L0_conv_w_conv).reshape(1, K * N), (P, K * N))
    w_up = by_channel(L0_conv_w_up).reshape(P, TILES, 2)
    w_guide = by_channel(np.asarray(L1_conv_w_guide).T)
    w_fuse = by_channel(L1_conv_w_fuse).transpose(2, 1, 0)
    bn = np.stack([by_channel(v) for v in (L1_conv_bn_gamma, L1_conv_bn_beta, L1_conv_bn_mean,
                                           L1_conv_bn_var)], axis=1)
    arrays = {"x": x, "w_down": w_down, "w_conv": w_conv, "w_up": w_up, "w_guide": w_guide,
              "w_fuse": w_fuse, "bn": bn, "consts": shape_constants()}
    arrays = {k: np.ascontiguousarray(v) for k, v in arrays.items()}
    nc = bacc.Bacc("TRN2", target_bir_lowering=False, num_devices=1)
    args = [nc.dram_tensor(k, v.shape, mybir.dt.from_np(v.dtype), kind="ExternalInput").ap()
            for k, v in arrays.items()]
    args.append(nc.dram_tensor("out", (B, CH, H, W), F32, kind="ExternalOutput").ap())
    build(nc, *args)
    r = run_bass_kernel_spmd(nc, [arrays], core_ids=[0])
    return r.results[0]["out"]
```

```python
from contextlib import ExitStack

import concourse.bass as bass
import numpy as np
from concourse import mybir

F32 = mybir.dt.float32
BF16 = mybir.dt.bfloat16
ALU = mybir.AluOpType
ACT = mybir.ActivationFunctionType
AX = mybir.AxisListType
ds = bass.ds

P = 128
B, CH, H, W = 8, 512, 128, 128
HC, WC = H // 2, W // 2
PX = HC * WC
TILES = CH // 2 // P
XR = 16
CR = XR // 2
S = H // XR
U = S // 2
STEPS = TILES * S
CN = CR * WC
K, N = 8, 2
KM_ITERS, EM_ITERS = 10, 10
EPS, BN_EPS = 1e-6, 1e-5
CHUNKS = PX // P
BLK = 512
FEAT = 2 * K + 1

TAPS = [(i, ky, kx) for ky in (1, 2) for kx in (1, 0, 2) for i in range(2)] + \
    [(i, 0, kx) for kx in (0, 1, 2) for i in range(2)]
MAX_PE_TAPS = 14


def pe_taps(j, phase):
    return 9 if isinstance(j, int) and j == 0 else {"start": 12, "iterate": 14, "finish": 11}[phase]


def dve_taps(j, phase):
    return sorted(TAPS[pe_taps(j, phase):], key=lambda tap: tap[2] == 0)


C_ID, C_U, C_COEF, C_FIRST, C_LAST = 0, 128, 256, 384, 512
C_SEED, C_TRI, C_IOTA, C_PREF = 640, 656, 720, 728
C_ALL = 736

UP = (2 * HC) / (HC - 0.5)

PS_CONV, PS_T, PS_UP, PS_SMALL = 0, 1, 3, 7
SM_SUM, SM_Y1, SM_Y2 = 256, 320, 328


def shape_constants():
    def coords(n_in, n_out):
        at = np.linspace(0.0, n_in - 1.0, n_out).astype(np.float32)
        low = np.floor(at).astype(np.int64)
        return low, np.minimum(low + 1, n_in - 1), (at - low.astype(np.float32)).astype(np.float32)

    c = np.zeros((P, C_ALL), np.float32)
    c[:, C_ID:C_ID + P] = np.eye(P)
    x0, x1, fx = coords(WC, W)
    u = np.zeros((WC, W), np.float32)
    for w in range(W):
        u[x0[w], w] += np.float32(1) - fx[w]
        u[x1[w], w] += fx[w]
    c[:, C_U:C_U + W] = np.concatenate([u, u])
    y0, _, fy = coords(HC, H)
    for y in range(H):
        s, r = divmod(y, XR)
        low = CR * s + (r + 1) // 2 - 1
        pos = C_COEF + XR * s + (r - 1) % XR
        wts = {int(y0[y]): np.float32(1) - fy[y], int(y0[y]) + 1: fy[y]}
        assert all(row in (low, low + 1) or not v for row, v in wts.items())
        c[:WC, pos] = wts.get(low, 0)
        c[WC:, pos] = wts.get(low + 1, 0)
    c[0, C_FIRST:C_FIRST + P] = 1
    c[P - 1, C_LAST:C_LAST + P] = 1
    for k, ch in enumerate(np.round(np.linspace(0.0, TILES * P - 1.0, K)).astype(np.int64)):
        c[ch % P, C_SEED + K * (ch // P) + k] = 1
    c[:, C_TRI:C_TRI + K * K] = np.tril(np.ones((K, K)), -1).reshape(-1)
    c[:, C_IOTA:C_IOTA + K] = np.arange(K)
    c[:, C_PREF:C_PREF + K] = np.arange(K, 0, -1)
    return c


def build(nc, x, w_down, w_conv, w_up, w_guide, w_fuse, bn, consts, out):
    with ExitStack() as ctx:
        def sb(name, shape, dt=F32):
            return ctx.enter_context(nc.sbuf_tensor(name, shape, dt))

        def sem(name):
            return ctx.enter_context(nc.semaphore(name))

        conv = sb("conv", [P, 2, TILES * PX + WC])
        xin = sb("xin", [P, 2, 2, XR + 1, W])
        xres = sb("xres", [P, 2, 2, XR, W])
        interp = sb("interp", [P, XR, W])
        pairs = sb("pairs", [P, CR + 1, P])
        stage = sb("stage", [P, CR + 2, WC])
        taps = sb("taps", [P, TILES, MAX_PE_TAPS, P])
        junk = sb("junk", [P, XR * W], BF16)
        cst = sb("cst", [P, C_ALL])
        ones = sb("ones", [P, P])
        wd = sb("wd", [P, TILES, 18])
        wc = sb("wc", [P, K, N])
        wu = sb("wu", [P, TILES, 2])
        wg = sb("wg", [P, TILES * 2, P])
        wf = sb("wf", [P, TILES * 2, P])
        bnp = sb("bnp", [P, 4, TILES * 2])
        inv_std = sb("inv_std", [P, TILES * 2])
        lo = sb("lo", [P, TILES])
        hi = sb("hi", [P, TILES])
        xnorm = sb("xnorm", [P, 2, TILES, P])
        xnormT = sb("xnormT", [P, 2, TILES * P])
        gram = sb("gram", [P, TILES, TILES * P])
        gdiag = sb("gdiag", [P, P])
        sq = sb("sq", [P, TILES])
        cent = sb("cent", [P, TILES, K])
        dots = sb("dots", [P, TILES, K])
        dist = sb("dist", [P, TILES, K])
        kt = sb("kt", [P, TILES, K])
        kbest = sb("kbest", [P, TILES])
        member = sb("member", [P, TILES, K])
        member_n = sb("member_n", [P, TILES, K])
        cnt = sb("cnt", [P, 3, K])
        kstat = sb("kstat", [K, PX // BLK, 6])
        kmv = sb("kmv", [K, 2])
        kvd = sb("kvd", [K, K])
        kv = sb("kv", [P, K])
        klt = sb("klt", [P, K, K])
        keq = sb("keq", [P, K, K])
        rank = sb("rank", [P, K])
        sorted_member = sb("sorted_member", [P, TILES, K])
        mean_w = sb("mean_w", [P, TILES, K])
        feat = sb("feat", [P, CHUNKS, FEAT])
        dmean = sb("dmean", [P, K])
        prod = sb("prod", [P, N, FEAT, CHUNKS])
        mu = sb("mu", [P, N, 2 * K])
        mu2 = sb("mu2", [P, N, K])
        varw = sb("varw", [P, N, K + 1])
        logs = sb("logs", [P, N, K + 1])
        ivar = sb("ivar", [P, N, K])
        coef = sb("coef", [P, N, 2 * K])
        cdiff = sb("cdiff", [P, 2 * K])
        lterm = sb("lterm", [P, N, K + 1])
        ldiff = sb("ldiff", [P, K + 1])
        lconst = sb("lconst", [P, 1])
        odds = sb("odds", [P, CHUNKS])
        logp = sb("logp", [P, N, CHUNKS])
        esum = sb("esum", [P, CHUNKS])
        resp = sb("resp", [P, N, CHUNKS])
        part = sb("part", [P, N, FEAT])
        rn = sb("rn", [P, N])
        small = sb("small", [P, 8, K])
        xsum = sb("xsum", [P, 2, TILES, 2, S])
        csum = sb("csum", [P, TILES, S])
        cedge = sb("cedge", [P, 4, TILES])
        cmean = sb("cmean", [P, TILES])
        gate = sb("gate", [P, TILES])
        gt = sb("gt", [P, TILES, K])
        chmean = sb("chmean", [P, TILES, 2])
        squeeze = sb("squeeze", [P, 1])
        scale = sb("scale", [P, 2, TILES * 2])
        shift = sb("shift", [P, 2, TILES * 2])
        ps = ctx.enter_context(nc.psum_tensor("ps", [P, 8, 512], F32))

        ident = cst[:, C_ID:C_ID + P]

        passed = sem("passed")
        tables_in = sem("tables_in")
        setup_in = sem("setup_in")
        taps_ready = sem("taps_ready")
        bn_var = sem("bn_var")
        bn_root = sem("bn_root")
        x_in = [sem(f"x_in{h}") for h in range(2)]
        xres_in = [[sem(f"xres_in{h}{i}") for i in range(2)] for h in range(2)]
        stored = [[sem(f"stored{h}{i}") for i in range(2)] for h in range(2)]
        halo = sem("halo")
        conv_ps = sem("conv_ps")
        conv_taken = sem("conv_taken")
        conv_done = sem("conv_done")
        xsummed = sem("xsummed")
        staged = sem("staged")
        tp = [sem(f"tp{i}") for i in range(3)]
        tc = [sem(f"tc{i}") for i in range(3)]
        interp_ready = sem("interp_ready")
        up_ps = [sem(f"up_ps{i}") for i in range(2)]
        up_taken = [sem(f"up_taken{i}") for i in range(2)]
        shifted = [sem(f"shifted{i}") for i in range(2)]
        result = [sem(f"result{i}") for i in range(2)]
        km_x = sem("km_x")
        km_t = [sem(f"km_t{h}") for h in range(2)]
        km_c = [sem(f"km_c{h}") for h in range(2)]
        km_g = sem("km_g")
        km_dve = sem("km_dve")
        km_pe = sem("km_pe")
        km_done = sem("km_done")
        v_ps = sem("v_ps")
        em_stat = sem("em_stat")
        em_stat_ps = sem("em_stat_ps")
        em_var = sem("em_var")
        em_logs = sem("em_logs")
        em_logp = sem("em_logp")
        em_exp = sem("em_exp")
        em_part = sem("em_part")
        em_sum = sem("em_sum")
        fin_dve = sem("fin_dve")
        fin_act = sem("fin_act")
        fin_pe = sem("fin_pe")
        params = sem("params")

        TABLE_DMAS, SETUP_DMAS = 2, 5
        xv = x.rearrange("b (t c i) (s r) w -> b t c i s (r w)", t=TILES, i=2, r=XR)
        ov = out.rearrange("b (t c i) (s r) w -> b t c i s (r w)", t=TILES, i=2, r=XR)

        def dram(view, b, t, s):
            return view[ds(b, 1), t, :, :, ds(s, 1), :].rearrange("a c i s f -> c (a i) (s f)")

        def dram_channel(view, b, t, s, i):
            return view[ds(b, 1), t, :, i, ds(s, 1), :].rearrange("a c s f -> c (a s f)")

        def stages(eng, stage_body):
            stage_body(0, 0, True, False, False)
            stage_body(1, 1, True, True, False)
            with eng.Fori(1, B // 2) as jj:
                for p in range(2):
                    stage_body(2 * jj + p, p, True, True, True)
            stage_body(B, 0, False, True, True)
            stage_body(B + 1, 1, False, False, True)

        def runs(em, eng, body):
            if not em:
                for t in range(TILES):
                    with eng.Fori(0, U) as u:
                        body(t, u, "none", 0)
                return
            body(0, 0, "start", 0)
            with eng.Fori(1, U) as u:
                body(0, u, "iterate", 2 * u - 2)
            with eng.Fori(0, 2) as u:
                body(1, u, "iterate", 2 * u + 2 * (U - 1))
            for u in range(2, U):
                body(1, u, "finish", 0)

        free_from_start = {"tensor": [*tp, *up_ps], "scalar": tc,
                           "vector": [conv_taken, *up_taken]}

        def wait_all(eng, *waits):
            waits = [(s_, v if isinstance(v, int) else eng.snap(v)) for s_, v in waits]
            for s_, v in waits:
                eng.wait_ge(s_, v)
            eng.sem_inc(passed)

        def diagonals(eng, t):
            for n, (i, ky, kx) in enumerate(TAPS[:MAX_PE_TAPS]):
                k = 9 * i + 3 * ky + kx
                if eng is nc.scalar:
                    eng.activation(taps[:, t, n, :], ident, ACT.Copy, scale=wd[:, t, k:k + 1])
                else:
                    eng.tensor_scalar(taps[:, t, n, :], ident, wd[:, t, k:k + 1], None, ALU.mult)
            eng.drain().then_inc(taps_ready, 1)

        block = ctx.enter_context(nc.Block())

        @block.sync
        def _(sp):
            sp.dma_start(cst[:, :], consts).then_inc(tables_in, 16)
            sp.dma_start(wd[:, :, :], w_down).then_inc(tables_in, 16)

            def load(b, t, s, h):
                sp.dma_start(xin[:, h, :, 1:XR + 1, :].rearrange("c i r w -> c i (r w)"),
                             dram(xv, b, t, s)).then_inc(x_in[h], 16)

            def load_again(b, t, s, h, i):
                sp.dma_start(xres[:, h, i, :, :].rearrange("c r w -> c (r w)"),
                             dram_channel(xv, b, t, s, i)).then_inc(xres_in[h][i], 16)

            load(0, 0, 0, 0)
            load(0, 0, 1, 1)
            for tile, src in ((wc[:, :, :].rearrange("c k n -> c (k n)"), w_conv), (wu[:, :, :], w_up),
                              (wg[:, :, :], w_guide), (wf[:, :, :], w_fuse), (bnp[:, :, :], bn)):
                sp.dma_start(tile, src).then_inc(setup_in, 16)

            def stage_body(j, do_conv, do_out, more_conv=True, more_out=True):
                def step(t, u, h, nb, nt, nu):
                    g = STEPS * j + S * t + 2 * u + h
                    o = g - 2 * STEPS
                    if do_conv and (nb == 0 or more_conv):
                        wait_all(sp,
                                 (conv_ps, g + 1),
                                 (xsummed, g + 1),
                                 (conv_done, g + 1))
                        wait_all(sp, (halo, g + 2))
                        load(j + nb, nt, 2 * nu + h, h)
                    if do_out:
                        for i in range(2):
                            sp.wait_ge(result[i], o + 1)
                            sp.dma_start(dram_channel(ov, j - 2, t, 2 * u + h, i),
                                         xres[:, h, i, :, :].rearrange("c r w -> c (r w)")) \
                                .then_inc(stored[h][i], 16)
                        if nb == 0 or more_out:
                            for i in range(2):
                                wait_all(sp, (stored[h][i],
                                              16 * (STEPS // 2 * (j - 2) + U * t + u + 1)))
                                load_again(j - 2 + nb, nt, 2 * nu + h, h, i)

                for t in range(TILES):
                    with sp.Fori(0, U - 1) as u:
                        for h in range(2):
                            step(t, u, h, 0, t, u + 1)
                    for h in range(2):
                        step(t, U - 1, h, *((0, t + 1, 0) if t + 1 < TILES else (1, 0, 0)))

            stage_body(0, True, False)
            stage_body(1, True, False)
            sp.wait_ge(km_done, 1)
            for h in range(2):
                for i in range(2):
                    load_again(0, 0, h, h, i)
            with sp.Fori(1, B // 2 - 1) as jj:
                for p in range(2):
                    stage_body(2 * jj + p, True, True)
            stage_body(B - 2, True, True)
            stage_body(B - 1, True, True, more_conv=False)
            stage_body(B, False, True)
            stage_body(B + 1, False, True, more_out=False)
            for h in range(2):
                for i in range(2):
                    sp.wait_ge(stored[h][i], 16 * B * STEPS // 2)

        @block.gpsimd
        def _(pool):
            pool.memset(ones[:, :], 1.0)
            pool.memset(feat[:, :, 2 * K], 1.0)
            pool.memset(stage[:, CR, :], 0.0)
            for p in range(2):
                pool.memset(conv[:, p, TILES * PX:], 0.0)
            pool.drain()
            pool.wait_ge(tables_in, 16 * TABLE_DMAS)
            diagonals(pool, 0)

            def halo_row(g, h, prev_count):
                wait_all(pool,
                         (conv_done, g - 1),
                         (x_in[1 - h], prev_count))
                pool.tensor_copy(xin[:, h, :, 0, :], xin[:, 1 - h, :, XR, :]).then_inc(halo, 1)

            def halo_zero(g):
                if not (isinstance(g, int) and g == 0):
                    wait_all(pool,
                             (conv_done, g - 1))
                pool.memset(xin[:, 0, :, 0, :], 0.0).then_inc(halo, 1)

            def stage_body(j, p, do_conv, do_em, do_out):
                def halos(t, u, top):
                    g = STEPS * j + S * t + 2 * u
                    landed = 8 * (STEPS * j + S * t) + 16 * u
                    if top:
                        halo_zero(g)
                    else:
                        halo_row(g, 0, landed)
                    halo_row(g + 1, 1, landed + 16)

                def rows(t, u, h):
                    o = STEPS * (j - 2) + S * t + 2 * u + h
                    wait_all(pool,
                             (tp[2], o + 1))
                    pool.tensor_copy(stage[:, 0, :], stage[:, CR, :])
                    pool.drain()
                    pool.tensor_copy(stage[:, 1:, :],
                                     conv[:, p, ds(t * PX + CN * (2 * u + h), CN + WC)]
                                     .rearrange("c (r w) -> c r w", w=WC)).then_inc(staged, 1)

                def weights(t, u, h):
                    o = STEPS * (j - 2) + S * t + 2 * u + h
                    pool.wait_ge(up_ps[1], o + 1)
                    pool.tensor_tensor(
                        interp[:, :, :],
                        cst[:, ds(C_COEF + XR * (2 * u + h), XR)].unsqueeze(2).to_broadcast([P, XR, W]),
                        cst[:, C_U:C_U + W].unsqueeze(1).to_broadcast([P, XR, W]),
                        ALU.mult).then_inc(interp_ready, 1)

                def round_(t, u, top):
                    if not do_out:
                        halos(t, u, top)
                        return
                    rows(t, u, 0)
                    if do_conv:
                        g = STEPS * j + S * t + 2 * u
                        landed = 8 * (STEPS * j + S * t) + 16 * u
                        if top:
                            halo_zero(g)
                        else:
                            halo_row(g, 0, landed)
                    weights(t, u, 0)
                    rows(t, u, 1)
                    if do_conv:
                        halo_row(g + 1, 1, landed + 16)
                    weights(t, u, 1)

                if do_out:
                    pool.wait_ge(conv_done, STEPS * (j - 1))
                for t in range(TILES):
                    round_(t, 0, True)
                    with pool.Fori(1, U) as u:
                        round_(t, u, False)

            stage_body(0, 0, True, False, False)
            stage_body(1, 1, True, True, False)
            pool.wait_ge(km_done, 1)
            with pool.Fori(1, B // 2) as jj:
                for p in range(2):
                    stage_body(2 * jj + p, p, True, True, True)
            stage_body(B, 0, False, True, True)
            stage_body(B + 1, 1, False, False, True)

        @block.scalar
        def _(act):
            for free in free_from_start["scalar"]:
                act.sem_inc(free)
            act.wait_ge(tables_in, 16 * TABLE_DMAS)
            diagonals(act, 1)

            def k_means():
                def copy_round(q):
                    for h in range(2):
                        act.wait_ge(km_t[h], q + 1)
                        if not (isinstance(q, int) and q == 0):
                            act.wait_ge(km_g, q)
                        act.activation(xnormT[:, h, :], ps[:, PS_T + h, 0:TILES * P], ACT.Copy) \
                            .then_inc(km_c[h], 1)
                copy_round(0)
                with act.Fori(1, CHUNKS // 2) as q:
                    copy_round(q)

            def stage_body(j, p, do_conv, do_em, do_out):
                def step(t, u, h, phase, em):
                    g = STEPS * j + S * t + 2 * u + h
                    o = g - 2 * STEPS
                    if do_out:
                        act.wait_ge(up_ps[1], o + 1)
                        act.wait_ge(tp[0], o + 2)
                        act.activation(pairs[:, CR, :], ps[:, PS_CONV, 0:P], ACT.Copy).then_inc(tc[0], 1)
                        for i in range(2):
                            act.wait_ge(tp[1 + i], o + 2)
                            act.activation(pairs[:, 4 * i:4 * i + 4, :].rearrange("c r w -> c (r w)"),
                                           ps[:, PS_T + i, :], ACT.Copy).then_inc(tc[1 + i], 1)
                    if phase == "iterate":
                        e = EM_ITERS * (j - 1) + em + h
                        act.wait_ge(em_var, (EM_ITERS + 1) * (j - 1) + em + h + 1)
                        act.activation(logs[:, :, :], varw[:, :, :], ACT.Ln).then_inc(em_logs, 1)
                        act.wait_ge(em_logp, e + 1)
                        for n in range(N):
                            r = act.activation(resp[:, n, :], logp[:, n, :], ACT.Exp,
                                               scale=-1.0 if n == 0 else 1.0)
                        r.then_inc(em_exp, 1)
                    if phase == "finish" and (u, h) == (2, 0):
                        act.wait_ge(fin_dve, 3 * (j - 1) + 1)
                        act.activation(small[:, 3, :], small[:, 2, :], ACT.Exp, scale=-1.0) \
                            .then_inc(fin_act, 1)
                    if do_out:
                        for i in range(2):
                            act.wait_ge(xres_in[h][i], 8 * (STEPS * (j - 2) + S * t) + 16 * u + 16)
                            c = xres[:, h, i, :, :].rearrange("c r w -> c (r w)")
                            act.activation(c, c, ACT.Identity, bias=shift[:, p, 2 * t + i:2 * t + i + 1]) \
                                .then_inc(shifted[i], 1)
                    if do_conv:
                        act.wait_ge(x_in[h], 8 * (STEPS * j + S * t) + 16 * u + 16)
                        for i in range(2):
                            act.activation(junk[:, :], xin[:, h, i, 1:, :].rearrange("c r w -> c (r w)"),
                                           ACT.Copy, accum_out=xsum[:, p, t, i, ds(2 * u + h, 1)])
                            d = act.drain()
                        d.then_inc(xsummed, 1)
                    if do_em and t == 0:
                        if phase == "start" and h == 0:
                            act.wait_ge(conv_done, STEPS * j)
                        for tile in range(TILES):
                            act.activation(junk[:, 0:CN],
                                           conv[:, 1 - p, ds(tile * PX + CN * (2 * u + h), CN)],
                                           ACT.Copy, accum_out=csum[:, tile, ds(2 * u + h, 1)])
                            act.drain()

                def round_(t, u, phase, em):
                    for h in range(2):
                        step(t, u, h, phase, em)

                if do_out:
                    act.wait_ge(params, j - 1)
                runs(do_em, act, round_)

            stage_body(0, 0, True, False, False)
            act.wait_ge(bn_var, 1)
            act.activation(inv_std[:, :], inv_std[:, :], ACT.Sqrt).then_inc(bn_root, 1)
            act.preload_act_table_set("natural_log_exp_and_others")
            k_means()
            stage_body(1, 1, True, True, False)
            with act.Fori(1, B // 2) as jj:
                for p in range(2):
                    stage_body(2 * jj + p, p, True, True, True)
            stage_body(B, 0, False, True, True)
            stage_body(B + 1, 1, False, False, True)

        @block.tensor
        def _(pe):
            for free in free_from_start["tensor"]:
                pe.sem_inc(free)
            pe.wait_ge(taps_ready, TILES)

            def k_means():
                def gram_round(q, first, last):
                    for h in range(2):
                        pe.wait_ge(km_x, 2 * q + h + 1)
                        if not first:
                            pe.wait_ge(km_c[h], q)
                        for t in range(TILES):
                            m = pe.transpose(ps[:, PS_T + h, t * P:(t + 1) * P], xnorm[:, h, t, :], ident)
                        m.then_inc(km_t[h], 1)
                    for h in range(2):
                        pe.wait_ge(km_c[h], q + 1)
                        for a in range(TILES):
                            m = pe.matmul(ps[:, PS_UP + a, 0:TILES * P], xnormT[:, h, a * P:(a + 1) * P],
                                          xnormT[:, h, :], start=first and h == 0, stop=last and h == 1)
                    m.then_inc(km_g, 1)
                gram_round(0, True, False)
                with pe.Fori(1, CHUNKS // 2 - 1) as q:
                    gram_round(q, False, False)
                gram_round(CHUNKS // 2 - 1, False, True)

                def over_channels(col, weights, values, n):
                    pe.wait_ge(km_dve, n + 1)
                    for t in range(TILES):
                        m = pe.matmul(ps[:, PS_SMALL, col:col + K], weights(t), values[:, t, :],
                                      start=t == 0, stop=t == TILES - 1)
                    return m

                with pe.Fori(0, KM_ITERS + 1) as it:
                    for a in range(TILES):
                        m = over_channels(K * a, lambda t: gram[:, t, a * P:(a + 1) * P], cent, 3 * it)
                    m.then_inc(km_pe, 1)
                    over_channels(2 * K, lambda t: ones[:, :], kt, 3 * it + 1).then_inc(km_pe, 1)
                    over_channels(3 * K, lambda t: ones[:, :], member, 3 * it + 2).then_inc(km_pe, 1)
                n = 3 * (KM_ITERS + 1)
                pe.wait_ge(km_dve, n + 1)
                for c in range(PX // BLK):
                    if c >= 2:
                        pe.wait_ge(km_dve, n + c)
                    for t in range(TILES):
                        m = pe.matmul(ps[0:K, PS_T + c % 2, :], member_n[:, t, :],
                                      conv[:, 0, t * PX + BLK * c:t * PX + BLK * (c + 1)],
                                      start=t == 0, stop=t == TILES - 1)
                    m.then_inc(km_pe, 1)
                n += PX // BLK + 2
                pe.wait_ge(km_dve, n)
                pe.matmul(ps[:, PS_SMALL, 4 * K:5 * K], ones[0:K, :], kvd[:, :], start=True, stop=True) \
                    .then_inc(km_pe, 1)
                pe.wait_ge(km_done, 1)

            def means(p, blocks):
                per = CN // P
                for c in range(per * blocks[0], per * blocks[1]):
                    for t in range(TILES):
                        m = pe.matmul(ps[:, PS_SMALL, c * K:(c + 1) * K],
                                      conv[:, p, t * PX + c * P:t * PX + (c + 1) * P],
                                      mean_w[:, t, :], start=t == 0, stop=t == TILES - 1)
                return m

            def next_means(j, p, u, h):
                if (u, h) == (2, 0):
                    pe.wait_ge(fin_dve, 3 * (j - 1) + 1)
                elif (u, h) == (3, 0):
                    pe.wait_ge(fin_dve, 3 * (j - 1) + 3)
                elif (u, h) == (3, 1):
                    pe.wait_ge(params, j)
                blocks = {(2, 0): (0, 2), (2, 1): (2, 4), (3, 0): (4, 6), (3, 1): (6, S - 1)}[u, h]
                pe.wait_ge(conv_done, STEPS * j + S + blocks[1])
                means(p, blocks)

            def mixture_mean(b):
                pe.wait_ge(em_stat, 2 * b + 1)
                pe.matmul(ps[:, PS_SMALL, SM_SUM:SM_SUM + K], ones[:, :], part[:, 0, 0:K],
                          start=True, stop=True).then_inc(em_stat_ps, 1)

            def mixture_start(b):
                pe.wait_ge(em_stat, 2 * b + 2)
                for n, (weights, values) in enumerate((
                        (cst[:, C_FIRST:C_FIRST + P], feat[:, 0, 0:K]),
                        (cst[:, C_LAST:C_LAST + P], feat[:, CHUNKS - 1, 0:K]),
                        (ones[:, :], part[:, 0, 0:K]))):
                    m = pe.matmul(ps[:, PS_SMALL, SM_SUM + n * K:SM_SUM + (n + 1) * K], weights, values,
                                  start=True, stop=True)
                m.then_inc(em_stat_ps, 1)

            def excite_in(b):
                pe.wait_ge(fin_dve, 3 * b + 2)
                for n in range(2 * TILES):
                    m = pe.matmul(ps[:, PS_SMALL, SM_Y1:SM_Y1 + 1], wg[:, n, :],
                                  chmean[:, :, :].rearrange("c t i -> c (t i)")[:, n:n + 1],
                                  start=n == 0, stop=n == 2 * TILES - 1)
                m.then_inc(fin_pe, 1)

            def excite_out(b):
                pe.wait_ge(fin_dve, 3 * b + 3)
                for n in range(2 * TILES):
                    m = pe.matmul(ps[:, PS_SMALL, SM_Y2 + n:SM_Y2 + n + 1], wf[:, n, :],
                                  squeeze[:, :], start=True, stop=True)
                m.then_inc(fin_pe, 1)

            def stage_body(j, p, do_conv, do_em, do_out):
                def step(t, u, h, phase, em):
                    g = STEPS * j + S * t + 2 * u + h
                    o = g - 2 * STEPS
                    if do_out:
                        pe.wait_ge(staged, o + 1)
                        pe.wait_ge(conv_taken, g + 1 if do_conv else B * STEPS + 1)
                        pe.transpose(ps[:, PS_CONV, 0:P],
                                     stage[:, CR:CR + 2, :].rearrange("c r w -> c (r w)"), ident) \
                            .then_inc(tp[0], 1)
                        for i in range(2):
                            pe.wait_ge(tc[1 + i], o + 1)
                            for m in range(4):
                                k = 4 * i + m
                                mm = pe.transpose(ps[:, PS_T + i, m * P:(m + 1) * P],
                                                  stage[:, k:k + 2, :].rearrange("c r w -> c (r w)"), ident)
                            mm.then_inc(tp[1 + i], 1)
                    if phase == "start" and h == 1:
                        mixture_mean(j - 1)
                    if do_conv:
                        pe.wait_ge(x_in[h], 8 * (STEPS * j + S * t) + 16 * u + 16)
                        pe.wait_ge(conv_taken, g + 1)
                        if do_out:
                            pe.wait_ge(tc[0], o + 2)
                        acc = ps[:, PS_CONV, :].rearrange("c (r w) -> c r w", w=WC)
                        count = pe_taps(j, phase)
                        for n, (i, ky, kx) in enumerate(TAPS[:count]):
                            rows = slice(ky, ky + XR - 1, 2)
                            last = n == count - 1
                            if ky == 0 and TAPS[n - 1][1] != 0:
                                pe.wait_ge(halo, g + 1)
                            if kx == 0:
                                mm = pe.matmul(acc[:, :, 1:], taps[:, t, n, :],
                                               xin[:, h, i, rows, 1:W - 2:2], start=n == 0, stop=last)
                            else:
                                mm = pe.matmul(acc, taps[:, t, n, :],
                                               xin[:, h, i, rows, kx - 1:W:2], start=n == 0, stop=last)
                        mm.then_inc(conv_ps, 1)
                    if phase == "start":
                        if h == 0:
                            pe.wait_ge(conv_done, STEPS * j)
                            first = 0 if isinstance(j, int) and j == 1 else S - 1
                            means(1 - p, (first, S)).then_inc(v_ps, 1)
                        else:
                            mixture_start(j - 1)
                    if phase == "finish":
                        if do_conv:
                            next_means(j, p, u, h)
                        if (u, h) == (2, 1):
                            excite_in(j - 1)
                        elif (u, h) == (3, 0):
                            excite_out(j - 1)
                    def mixture_sums():
                        e = EM_ITERS * (j - 1) + em + h
                        pe.wait_ge(em_part, e + 1)
                        pe.matmul(ps[:, PS_SMALL, SM_SUM:SM_SUM + N * FEAT], ones[:, :],
                                  part[:, :, :].rearrange("c n k -> c (n k)"),
                                  start=True, stop=True).then_inc(em_sum, 1)

                    if phase == "iterate" and do_conv:
                        mixture_sums()
                    if do_out:
                        pe.wait_ge(interp_ready, o + 1)
                        for i in range(3):
                            pe.wait_ge(tc[i], o + 2)
                        for half, ms in ((0, (1, 2, 3, 4)), (1, (5, 6, 7, 8, 0))):
                            pe.wait_ge(up_taken[half], o + 1)
                            for m in ms:
                                pos, n = (2 * m - 2, 2) if 0 < m < CR else (2 * CR - 2, 1) if m else (2 * CR - 1, 1)
                                mm = pe.matmul(ps[:, PS_UP + pos // 4, (pos % 4) * W:(pos % 4 + n) * W],
                                               pairs[:, m, :],
                                               interp[:, pos:pos + n, :].rearrange("c r w -> c (r w)"),
                                               start=True, stop=True)
                            mm.then_inc(up_ps[half], 1)
                    if phase == "iterate" and not do_conv:
                        mixture_sums()

                def round_(t, u, phase, em):
                    for h in range(2):
                        step(t, u, h, phase, em)

                runs(do_em, pe, round_)

            stage_body(0, 0, True, False, False)
            k_means()
            stage_body(1, 1, True, True, False)
            with pe.Fori(1, B // 2) as jj:
                for p in range(2):
                    stage_body(2 * jj + p, p, True, True, True)
            stage_body(B, 0, False, True, True)
            stage_body(B + 1, 1, False, False, True)

        @block.vector
        def _(dve):
            def tt(out_, a, b, op):
                dve.tensor_tensor(out_, a, b, op)
                return dve.drain()

            def tsc(out_, a, s1, s2, op0, op1=ALU.bypass):
                dve.tensor_scalar(out_, a, s1, s2, op0, op1) if s2 is not None else \
                    dve.tensor_scalar(out_, a, s1, None, op0)
                return dve.drain()

            def stt(out_, a, s, b, op0, op1):
                dve.scalar_tensor_tensor(out_, a, s, b, op0, op1)
                return dve.drain()

            def red(out_, a, op=ALU.add):
                dve.tensor_reduce(out_, a, AX.X, op)
                return dve.drain()

            def recip(out_, a):
                dve.reciprocal(out_, a)
                return dve.drain()

            for free in free_from_start["vector"]:
                dve.sem_inc(free)
            dve.wait_ge(tables_in, 16 * TABLE_DMAS)

            def k_means():
                both = conv[:, 0, 0:TILES * PX].rearrange("c (t x) -> c t x", t=TILES)
                dve.tensor_reduce(lo[:, :], both, AX.X, ALU.min)
                red(hi[:, :], both, ALU.max)
                tt(hi[:, :], hi[:, :], lo[:, :], ALU.subtract)
                tsc(hi[:, :], hi[:, :], 1e-12, None, ALU.max)
                recip(hi[:, :], hi[:, :])

                def normalise(q):
                    for h in range(2):
                        if not (isinstance(q, int) and q == 0):
                            dve.wait_ge(km_t[h], q)
                        for t in range(TILES):
                            m = dve.tensor_scalar(xnorm[:, h, t, :],
                                                  conv[:, 0, ds(t * PX + P * (2 * q + h), P)],
                                                  lo[:, t:t + 1], hi[:, t:t + 1], ALU.subtract, ALU.mult)
                        m.then_inc(km_x, 1)
                normalise(0)
                with dve.Fori(1, CHUNKS // 2) as q:
                    normalise(q)

                dve.wait_ge(km_g, CHUNKS // 2)
                for a in range(TILES):
                    dve.tensor_copy(gram[:, a, :], ps[:, PS_UP + a, 0:TILES * P])
                dve.drain()
                for a in range(TILES):
                    tt(gdiag[:, :], gram[:, a, a * P:(a + 1) * P], ident, ALU.mult)
                    red(sq[:, a:a + 1], gdiag[:, :])
                dve.tensor_copy(cent[:, :, :].rearrange("c t k -> c (t k)"),
                                cst[:, C_SEED:C_SEED + TILES * K]).then_inc(km_dve, 1)

                def wide(v, shape=(P, TILES, K)):
                    return v.unsqueeze(1 if v.shape[1] == K else 2).to_broadcast(list(shape))

                prefer = cst[:, C_PREF:C_PREF + K]
                with dve.Fori(0, KM_ITERS + 1) as it:
                    dve.wait_ge(km_pe, 3 * it + 1)
                    dve.tensor_copy(dots[:, :, :].rearrange("c t k -> c (t k)"),
                                    ps[:, PS_SMALL, 0:TILES * K])
                    dve.drain()
                    tt(kt[:, :, :], dots[:, :, :], cent[:, :, :], ALU.mult).then_inc(km_dve, 1)
                    dve.wait_ge(km_pe, 3 * it + 2)
                    tt(dist[:, :, :], wide(ps[:, PS_SMALL, 2 * K:3 * K]), wide(sq[:, :]), ALU.add)
                    stt(dist[:, :, :].rearrange("c t k -> c (t k)"),
                        dots[:, :, :].rearrange("c t k -> c (t k)"), -2.0,
                        dist[:, :, :].rearrange("c t k -> c (t k)"), ALU.mult, ALU.add)
                    red(kbest[:, :], dist[:, :, :], ALU.min)
                    tt(dist[:, :, :], dist[:, :, :], wide(kbest[:, :]), ALU.is_equal)
                    tt(dist[:, :, :], dist[:, :, :], wide(prefer), ALU.mult)
                    red(kbest[:, :], dist[:, :, :], ALU.max)
                    tt(member[:, :, :], dist[:, :, :], wide(kbest[:, :]), ALU.is_equal) \
                        .then_inc(km_dve, 1)
                    dve.wait_ge(km_pe, 3 * it + 3)
                    tsc(cnt[:, 0, :], ps[:, PS_SMALL, 3 * K:4 * K], 1.0, None, ALU.max)
                    tsc(cnt[:, 2, :], ps[:, PS_SMALL, 3 * K:4 * K], 0.0, None, ALU.is_le)
                    recip(cnt[:, 1, :], cnt[:, 0, :])
                    tt(cent[:, :, :], cent[:, :, :], wide(cnt[:, 2, :]), ALU.mult)
                    tt(member_n[:, :, :], member[:, :, :], wide(cnt[:, 1, :]), ALU.mult)
                    tt(cent[:, :, :], cent[:, :, :], member_n[:, :, :], ALU.add).then_inc(km_dve, 1)
                for c in range(PX // BLK):
                    dve.wait_ge(km_pe, 3 * (KM_ITERS + 1) + c + 1)
                    dve.bn_stats(kstat[:, c, :], ps[0:K, PS_T + c % 2, :])
                    dve.drain().then_inc(km_dve, 1)
                dve.bn_aggr(kmv[:, :], kstat[:, :, :].rearrange("k c s -> k (c s)"))
                dve.drain()
                tsc(kvd[:, :], ident[0:K, 0:K], kmv[:, 1:2], None, ALU.mult).then_inc(km_dve, 1)
                dve.wait_ge(km_pe, 3 * (KM_ITERS + 1) + PX // BLK + 1)
                dve.tensor_copy(kv[:, :], ps[:, PS_SMALL, 4 * K:5 * K])
                dve.drain()
                other = kv[:, :].unsqueeze(1).to_broadcast([P, K, K])
                own = kv[:, :].unsqueeze(2).to_broadcast([P, K, K])
                tt(klt[:, :, :], other, own, ALU.is_lt)
                tt(keq[:, :, :], other, own, ALU.is_equal)
                tt(keq[:, :, :], keq[:, :, :], cst[:, C_TRI:C_TRI + K * K].rearrange("c (k m) -> c k m", k=K),
                   ALU.mult)
                tt(klt[:, :, :], klt[:, :, :], keq[:, :, :], ALU.add)
                red(rank[:, :], klt[:, :, :])
                tt(kt[:, :, :], member[:, :, :], wide(rank[:, :]), ALU.mult)
                red(kbest[:, :], kt[:, :, :])
                tt(sorted_member[:, :, :], wide(kbest[:, :]), wide(cst[:, C_IOTA:C_IOTA + K]), ALU.is_equal)
                red(kbest[:, :], member_n[:, :, :])
                tt(mean_w[:, :, :], sorted_member[:, :, :], wide(kbest[:, :]), ALU.mult).then_inc(km_done, 1)

            f_ck = feat[:, :, :]
            f_kc = feat[:, :, :].rearrange("p c k -> p k c")

            def mixture_mean():
                got = ps[:, PS_SMALL, 0:CHUNKS * K].rearrange("p (c k) -> p c k", k=K)
                dve.tensor_copy(f_ck[:, :, 0:K], got)
                dve.tensor_reduce(part[:, 0, 0:K], got.rearrange("p c k -> p k c"), AX.X, ALU.add)
                dve.drain().then_inc(em_stat, 1)

            def mixture_variance():
                tsc(dmean[:, :], ps[:, PS_SMALL, SM_SUM:SM_SUM + K], 1.0 / PX, None, ALU.mult)
                d = f_ck[:, :, 0:K]
                tt(d, d, dmean[:, :].unsqueeze(1).to_broadcast([P, CHUNKS, K]), ALU.subtract)
                tt(f_ck[:, :, K:2 * K], d, d, ALU.mult)
                red(part[:, 0, 0:K], f_kc[:, K:2 * K, :]).then_inc(em_stat, 1)

            def mixture_start():
                dve.tensor_copy(mu[:, :, 0:K], ps[:, PS_SMALL, SM_SUM:SM_SUM + N * K]
                                .rearrange("p (n k) -> p n k", n=N))
                for n in range(N):
                    dve.tensor_scalar(varw[:, n, 0:K], ps[:, PS_SMALL, SM_SUM + N * K:SM_SUM + (N + 1) * K],
                                      1.0 / PX, EPS, ALU.mult, ALU.add)
                    dve.memset(varw[:, n, K:K + 1], 1.0 / N)
                dve.drain().then_inc(em_var, 1)
                tt(mu2[:, :, :], mu[:, :, 0:K], mu[:, :, 0:K], ALU.mult)

            def em_expect(e):
                dve.reciprocal(ivar[:, :, :], varw[:, :, 0:K])
                dve.drain()
                dve.tensor_tensor(coef[:, :, 0:K], mu[:, :, 0:K], ivar[:, :, :], ALU.mult)
                dve.tensor_scalar(coef[:, :, K:2 * K], ivar[:, :, :], -0.5, None, ALU.mult)
                dve.tensor_tensor(lterm[:, :, 0:K], mu2[:, :, :], ivar[:, :, :], ALU.mult)
                dve.drain()
                tt(cdiff[:, :], coef[:, 1, :], coef[:, 0, :], ALU.subtract)
                terms = prod[:, 0, :, :].rearrange("p f c -> p (f c)")[:, 0:CHUNKS * 2 * K] \
                    .rearrange("p (c f) -> p c f", f=2 * K)
                dve.tensor_tensor(terms, f_ck[:, :, 0:2 * K],
                                  cdiff[:, :].unsqueeze(1).to_broadcast([P, CHUNKS, 2 * K]), ALU.mult)
                dve.wait_ge(em_logs, e + 1)
                dve.tensor_tensor(lterm[:, :, 0:K], lterm[:, :, 0:K], logs[:, :, 0:K], ALU.add)
                dve.tensor_scalar(lterm[:, :, K], logs[:, :, K], -2.0, float(K * np.log(2 * np.pi)),
                                  ALU.mult, ALU.add)
                dve.drain()
                dve.tensor_reduce(odds[:, :], terms, AX.X, ALU.add)
                dve.tensor_tensor(ldiff[:, :], lterm[:, 0, :], lterm[:, 1, :], ALU.subtract)
                dve.drain()
                red(lconst[:, :], ldiff[:, :])
                tsc(lconst[:, :], lconst[:, :], 0.5, None, ALU.mult)
                dve.tensor_scalar(logp[:, 0, :], odds[:, :], lconst[:, 0:1], 0.0, ALU.add, ALU.max)
                dve.tensor_scalar(logp[:, 1, :], odds[:, :], lconst[:, 0:1], 0.0, ALU.add, ALU.min)
                dve.drain().then_inc(em_logp, 1)

            def em_sums(e):
                dve.wait_ge(em_exp, e + 1)
                tt(esum[:, :], resp[:, 0, :], resp[:, 1, :], ALU.add)
                recip(esum[:, :], esum[:, :])
                tt(resp[:, :, :], resp[:, :, :], esum[:, :].unsqueeze(1).to_broadcast([P, N, CHUNKS]),
                   ALU.mult)
                for n in range(N):
                    dve.tensor_tensor(prod[:, n, :, :], f_kc,
                                      resp[:, n, :].unsqueeze(1).to_broadcast([P, FEAT, CHUNKS]), ALU.mult)
                dve.drain()
                red(part[:, :, :], prod[:, :, :, :]).then_inc(em_part, 1)

            def em_update(e):
                dve.wait_ge(em_sum, e + 1)
                sums = ps[:, PS_SMALL, SM_SUM:SM_SUM + N * FEAT].rearrange("p (n k) -> p n k", n=N)
                dve.tensor_scalar(varw[:, :, K], sums[:, :, 2 * K], 1.0 / PX, None, ALU.mult)
                recip(rn[:, :], sums[:, :, 2 * K])
                tt(mu[:, :, :], sums[:, :, 0:2 * K], rn[:, :].unsqueeze(2).to_broadcast([P, N, 2 * K]),
                   ALU.mult)
                tt(mu2[:, :, :], mu[:, :, 0:K], mu[:, :, 0:K], ALU.mult)
                tt(varw[:, :, 0:K], mu[:, :, K:2 * K], mu2[:, :, :], ALU.subtract)
                tsc(varw[:, :, 0:K], varw[:, :, 0:K], EPS, EPS, ALU.add, ALU.max).then_inc(em_var, 1)

            def conv_edges(q):
                rows = conv[:, q, 0:TILES * PX].rearrange("c (t h w) -> c t h w", t=TILES, w=WC)
                cols = conv[:, q, 0:TILES * PX].rearrange("c (t h w) -> c t w h", t=TILES, w=WC)
                dve.tensor_reduce(cedge[:, 0, :], rows[:, :, 0:HC:HC - 1, :], AX.XY, ALU.add)
                dve.tensor_reduce(cedge[:, 1, :], cols[:, :, 0:WC:WC - 1, :], AX.XY, ALU.add)
                dve.tensor_reduce(cedge[:, 2, :], rows[:, :, 0:HC:HC - 1, 0:WC:WC - 1], AX.XY, ALU.add)
                dve.drain()
                tt(cedge[:, 0, :], cedge[:, 0, :], cedge[:, 1, :], ALU.add)
                stt(cedge[:, 0, :], cedge[:, 2, :], -0.25, cedge[:, 0, :], ALU.mult, ALU.add)

            def order_components():
                le, gt_, z, s0, s1 = (small[:, i, :] for i in (0, 1, 2, 4, 5))
                dve.tensor_tensor(mu[:, :, 0:K], mu[:, :, 0:K],
                                  dmean[:, :].unsqueeze(1).to_broadcast([P, N, K]), ALU.add)
                tt(le, varw[:, 0, 0:K], varw[:, 1, 0:K], ALU.is_le)
                tsc(gt_, le, -1.0, 1.0, ALU.mult, ALU.add)
                for n, first, second in ((0, le, gt_), (1, gt_, le)):
                    dve.tensor_tensor(s0, first, mu[:, 0, 0:K], ALU.mult)
                    tt(s1, second, mu[:, 1, 0:K], ALU.mult)
                    tt(s0, s0, s1, ALU.add)
                    if n == 0:
                        tt(z, s0, wc[:, :, n], ALU.mult)
                    else:
                        tt(s0, s0, wc[:, :, n], ALU.mult)
                        tt(z, z, s0, ALU.add).then_inc(fin_dve, 1)

            def gate_and_means(q):
                s0 = small[:, 4, :]
                tsc(s0, small[:, 3, :], 1.0, None, ALU.add)
                recip(s0, s0)
                tt(gt[:, :, :], sorted_member[:, :, :], s0.unsqueeze(1).to_broadcast([P, TILES, K]), ALU.mult)
                dve.tensor_reduce(gate[:, :], gt[:, :, :], AX.X, ALU.add)
                dve.tensor_reduce(cmean[:, :], csum[:, :, :], AX.X, ALU.add)
                dve.tensor_reduce(chmean[:, :, :].rearrange("c t i -> c (t i)"),
                                  xsum[:, q, :, :, :].rearrange("c t i s -> c (t i) s"), AX.X, ALU.add)
                dve.drain()
                stt(cmean[:, :], cedge[:, 0, :], -0.25, cmean[:, :], ALU.mult, ALU.add)
                dve.tensor_scalar(cmean[:, :], cmean[:, :], UP * UP, None, ALU.mult)
                tsc(gate[:, :], gate[:, :], 1.0, None, ALU.add)
                new = scale[:, q, :].rearrange("c (t i) -> c t i", t=TILES)
                tt(new, wu[:, :, :], gate[:, :].unsqueeze(2).to_broadcast([P, TILES, 2]), ALU.mult)
                tt(gt[:, :, 0:2], new, cmean[:, :].unsqueeze(2).to_broadcast([P, TILES, 2]), ALU.mult)
                tt(chmean[:, :, :], chmean[:, :, :], gt[:, :, 0:2], ALU.add)
                tsc(chmean[:, :, :], chmean[:, :, :], 1.0 / (H * W), None, ALU.mult).then_inc(fin_dve, 1)

            def excite(q):
                y = small[:, 6, 0:2 * TILES]
                tt(y, ps[:, PS_SMALL, SM_Y2:SM_Y2 + 2 * TILES], bnp[:, 2, :], ALU.subtract)
                tt(y, y, inv_std[:, :], ALU.mult)
                tt(y, y, bnp[:, 0, :], ALU.mult)
                tt(y, y, bnp[:, 1, :], ALU.add)
                tsc(shift[:, q, :], y, 0.0, 6.0, ALU.max, ALU.min).then_inc(params, 1)

            def before_taps(b, q, u, h, phase, em):
                if phase == "start" and h == 1:
                    dve.wait_ge(em_stat_ps, 2 * b + 1)
                    mixture_variance()
                elif phase == "finish" and (u, h) == (2, 0):
                    order_components()
                    conv_edges(q)
                elif phase == "iterate":
                    em_expect(EM_ITERS * b + em + h)
                    em_sums(EM_ITERS * b + em + h)

            def after_output(b, q, u, h, phase, em):
                if phase == "start":
                    if h == 0:
                        dve.wait_ge(v_ps, b + 1)
                        mixture_mean()
                    else:
                        dve.wait_ge(em_stat_ps, 2 * b + 2)
                        mixture_start()
                elif phase == "finish":
                    if (u, h) == (2, 0):
                        dve.wait_ge(fin_act, b + 1)
                        gate_and_means(q)
                    elif (u, h) == (2, 1):
                        dve.wait_ge(fin_pe, 2 * b + 1)
                        tsc(squeeze[:, :], ps[:, PS_SMALL, SM_Y1:SM_Y1 + 1], 0.0, 6.0, ALU.max, ALU.min) \
                            .then_inc(fin_dve, 1)
                    elif (u, h) == (3, 0):
                        dve.wait_ge(fin_pe, 2 * b + 2)
                        excite(q)
                elif phase == "iterate":
                    em_update(EM_ITERS * b + em + h)

            def stage_body(j, p, do_conv, do_em, do_out):
                def step(t, u, h, phase, em):
                    g = STEPS * j + S * t + 2 * u + h
                    o = g - 2 * STEPS
                    before_taps(j - 1, 1 - p, u, h, phase, em)
                    if do_conv:
                        dve.wait_ge(x_in[h], 8 * (STEPS * j + S * t) + 16 * u + 16)
                        rows = conv[:, p, ds(t * PX + CN * (2 * u + h), CN)].rearrange(
                            "c (r w) -> c r w", w=WC)
                        acc = ps[:, PS_CONV, :].rearrange("c (r w) -> c r w", w=WC)
                        if do_out:
                            dve.wait_ge(staged, o + 1)
                            dve.wait_ge(conv_ps, g + 1)
                        dve.wait_ge(halo, g + 1)
                        for n, (i, ky, kx) in enumerate(dve_taps(j, phase)):
                            k = 9 * i + 3 * ky + kx
                            last = n == len(dve_taps(j, phase)) - 1
                            src = xin[:, h, i, ky:ky + XR - 1:2, 1:W - 2:2] if kx == 0 else \
                                xin[:, h, i, ky:ky + XR - 1:2, kx - 1:W:2]
                            to = rows[:, :, 1:] if kx == 0 else rows
                            if n > 0:
                                dve.scalar_tensor_tensor(to, src, wd[:, t, k:k + 1], to, ALU.mult, ALU.add)
                                d = dve.drain()
                            elif do_out:
                                dve.scalar_tensor_tensor(to, src, wd[:, t, k:k + 1], acc, ALU.mult, ALU.add)
                                dve.drain().then_inc(conv_taken, 1)
                            else:
                                dve.tensor_scalar(to, src, wd[:, t, k:k + 1], None, ALU.mult)
                                dve.drain()
                        if not do_out:
                            dve.wait_ge(conv_ps, g + 1)
                            dve.tensor_tensor(rows, rows, acc, ALU.add)
                            dve.drain().then_inc(conv_taken, 1)
                            d = dve.drain()
                        d.then_inc(conv_done, 1)
                    if do_out:
                        for i in range(2):
                            dve.wait_ge(shifted[i], o + 1)
                            for half in range(2):
                                if i == 0:
                                    dve.wait_ge(up_ps[half], o + 2)
                                sc = scale[:, p, 2 * t + i:2 * t + i + 1]
                                up = ps[:, PS_UP:PS_UP + 4, :].rearrange("c b n -> c (b n)")
                                spans = [(1, 9, 0)] if half == 0 else [(9, XR, CR), (0, 1, XR - 1)]
                                for r0, r1, pos in spans:
                                    dst = xres[:, h, i, r0:r1, :].rearrange("c r w -> c (r w)")
                                    m = dve.scalar_tensor_tensor(dst, up[:, pos * W:(pos + r1 - r0) * W],
                                                                 sc, dst, ALU.mult, ALU.add)
                                if i == 1:
                                    m.then_inc(up_taken[half], 1)
                            dve.drain().then_inc(result[i], 1)
                    after_output(j - 1, 1 - p, u, h, phase, em)

                def round_(t, u, phase, em):
                    for h in range(2):
                        step(t, u, h, phase, em)

                runs(do_em, dve, round_)

            stage_body(0, 0, True, False, False)
            dve.wait_ge(setup_in, 16 * SETUP_DMAS)
            tsc(inv_std[:, :], bnp[:, 3, :], BN_EPS, None, ALU.add).then_inc(bn_var, 1)
            k_means()
            dve.wait_ge(bn_root, 1)
            recip(inv_std[:, :], inv_std[:, :])
            stage_body(1, 1, True, True, False)
            with dve.Fori(1, B // 2) as jj:
                for p in range(2):
                    stage_body(2 * jj + p, p, True, True, True)
            stage_body(B, 0, False, True, True)
            stage_body(B + 1, 1, False, False, True)


def kernel(x, L0_conv_w_down, L0_conv_w_conv, L0_conv_w_up, L1_conv_w_guide, L1_conv_w_fuse,
           L1_conv_bn_gamma, L1_conv_bn_beta, L1_conv_bn_mean, L1_conv_bn_var):
    import concourse.bacc as bacc
    from concourse.bass_utils import run_bass_kernel_spmd

    def by_channel(v):
        v = np.asarray(v)
        v = v.reshape(TILES, P, 2, *v.shape[1:])
        return np.ascontiguousarray(np.moveaxis(v, 0, 1).reshape(P, TILES * 2, *v.shape[3:]))

    w_down = np.asarray(L0_conv_w_down).reshape(TILES, P, 18).transpose(1, 0, 2)
    w_conv = np.broadcast_to(np.asarray(L0_conv_w_conv).reshape(1, K * N), (P, K * N))
    w_up = by_channel(L0_conv_w_up).reshape(P, TILES, 2)
    w_guide = by_channel(np.asarray(L1_conv_w_guide).T)
    w_fuse = by_channel(L1_conv_w_fuse).transpose(2, 1, 0)
    bn = np.stack([by_channel(v) for v in (L1_conv_bn_gamma, L1_conv_bn_beta, L1_conv_bn_mean,
                                           L1_conv_bn_var)], axis=1)
    arrays = {"x": x, "w_down": w_down, "w_conv": w_conv, "w_up": w_up, "w_guide": w_guide,
              "w_fuse": w_fuse, "bn": bn, "consts": shape_constants()}
    arrays = {k: np.ascontiguousarray(v) for k, v in arrays.items()}
    nc = bacc.Bacc("TRN2", target_bir_lowering=False, num_devices=1)
    args = [nc.dram_tensor(k, v.shape, mybir.dt.from_np(v.dtype), kind="ExternalInput").ap()
            for k, v in arrays.items()]
    args.append(nc.dram_tensor("out", (B, CH, H, W), F32, kind="ExternalOutput").ap())
    build(nc, *args)
    r = run_bass_kernel_spmd(nc, [arrays], core_ids=[0])
    return r.results[0]["out"]
```

```python
from contextlib import ExitStack

import concourse.bass as bass
import numpy as np
from concourse import mybir

F32 = mybir.dt.float32
BF16 = mybir.dt.bfloat16
ALU = mybir.AluOpType
ACT = mybir.ActivationFunctionType
AX = mybir.AxisListType
ds = bass.ds

P = 128
B, CH, H, W = 8, 512, 128, 128
HC, WC = H // 2, W // 2
PX = HC * WC
TILES = CH // 2 // P
XR = 16
CR = XR // 2
S = H // XR
U = S // 2
STEPS = TILES * S
CN = CR * WC
K, N = 8, 2
KM_ITERS, EM_ITERS = 10, 10
EPS, BN_EPS = 1e-6, 1e-5
CHUNKS = PX // P
FEAT = 2 * K + 1

TAPS = [(i, ky, kx) for ky in (1, 2) for kx in (1, 0, 2) for i in range(2)] + \
    [(i, 0, kx) for kx in (0, 1, 2) for i in range(2)]
MAX_PE_TAPS = 14


def tap_shares(j, phase):
    if isinstance(j, int) and j < 2:
        tensor = {"none": 9, "start": 11, "iterate": 14, "finish": 9}[phase]
    else:
        tensor = {"start": 12, "iterate": 14, "finish": 11}[phase]
    return TAPS[:tensor], sorted(TAPS[tensor:], key=lambda tap: tap[2] == 0)


C_ID, C_U, C_COEF, C_FIRST, C_LAST = 0, 128, 256, 384, 512
C_SEED, C_TRI, C_IOTA, C_PREF = 640, 656, 720, 728
C_ALL = 736

UP = (2 * HC) / (HC - 0.5)

PS_CONV, PS_T, PS_UP, PS_GRAM, PS_SMALL = 0, 1, 3, 4, 7
SM_SUM, SM_Y1, SM_Y2 = 256, 320, 328


def shape_constants():
    def coords(n_in, n_out):
        at = np.linspace(0.0, n_in - 1.0, n_out).astype(np.float32)
        low = np.floor(at).astype(np.int64)
        return low, np.minimum(low + 1, n_in - 1), (at - low.astype(np.float32)).astype(np.float32)

    c = np.zeros((P, C_ALL), np.float32)
    c[:, C_ID:C_ID + P] = np.eye(P)
    x0, x1, fx = coords(WC, W)
    u = np.zeros((WC, W), np.float32)
    for w in range(W):
        u[x0[w], w] += np.float32(1) - fx[w]
        u[x1[w], w] += fx[w]
    c[:, C_U:C_U + W] = np.concatenate([u, u])
    y0, _, fy = coords(HC, H)
    for y in range(H):
        s, r = divmod(y, XR)
        low = CR * s + (r + 1) // 2 - 1
        pos = C_COEF + XR * s + (r - 1) % XR
        wts = {int(y0[y]): np.float32(1) - fy[y], int(y0[y]) + 1: fy[y]}
        assert all(row in (low, low + 1) or not v for row, v in wts.items())
        c[:WC, pos] = wts.get(low, 0)
        c[WC:, pos] = wts.get(low + 1, 0)
    c[0, C_FIRST:C_FIRST + P] = 1
    c[P - 1, C_LAST:C_LAST + P] = 1
    for k, ch in enumerate(np.round(np.linspace(0.0, TILES * P - 1.0, K)).astype(np.int64)):
        c[ch % P, C_SEED + K * (ch // P) + k] = 1
    c[:, C_TRI:C_TRI + K * K] = np.tril(np.ones((K, K)), -1).reshape(-1)
    c[:, C_IOTA:C_IOTA + K] = np.arange(K)
    c[:, C_PREF:C_PREF + K] = np.arange(K, 0, -1)
    return c


def build(nc, x, w_down, w_conv, w_up, w_guide, w_fuse, bn, consts, out):
    with ExitStack() as ctx:
        def sb(name, shape, dt=F32):
            return ctx.enter_context(nc.sbuf_tensor(name, shape, dt))

        def sem(name):
            return ctx.enter_context(nc.semaphore(name))

        conv = sb("conv", [P, 2, TILES * PX + WC])
        xin = sb("xin", [P, 2, 2, XR + 1, W])
        xres = sb("xres", [P, 2, 2, XR, W])
        interp = sb("interp", [P, XR, W])
        pairs = sb("pairs", [P, CR + 1, P])
        stage = sb("stage", [P, CR + 2, WC])
        taps = sb("taps", [P, TILES, MAX_PE_TAPS, P])
        junk = sb("junk", [P, XR * W], BF16)
        cst = sb("cst", [P, C_ALL])
        ones = sb("ones", [P, P])
        wd = sb("wd", [P, TILES, 18])
        wc = sb("wc", [P, K, N])
        wu = sb("wu", [P, TILES, 2])
        wg = sb("wg", [P, TILES * 2, P])
        wf = sb("wf", [P, TILES * 2, P])
        bnp = sb("bnp", [P, 4, TILES * 2])
        inv_std = sb("inv_std", [P, TILES * 2])
        lo = sb("lo", [P, TILES])
        hi = sb("hi", [P, TILES])
        xnorm = sb("xnorm", [P, 2, TILES, P])
        xnormT = sb("xnormT", [P, 2, TILES * P])
        gram = sb("gram", [P, TILES, TILES * P])
        gdiag = sb("gdiag", [P, P])
        sq = sb("sq", [P, TILES])
        dots = sb("dots", [P, TILES, K])
        dist = sb("dist", [P, TILES, K])
        kt = sb("kt", [P, TILES, K])
        kbest = sb("kbest", [P, TILES])
        member = sb("member", [P, TILES, K])
        member_n = sb("member_n", [P, TILES, K])
        cnt = sb("cnt", [P, 3, K])
        c2 = sb("c2", [P, 2, K])
        point_sq = sb("point_sq", [P, TILES, K])
        kpx = sb("kpx", [P, CHUNKS, K])
        kv = sb("kv", [P, K])
        klt = sb("klt", [P, K, K])
        keq = sb("keq", [P, K, K])
        rank = sb("rank", [P, K])
        sorted_member = sb("sorted_member", [P, TILES, K])
        mean_w = sb("mean_w", [P, TILES, K])
        feat = sb("feat", [P, CHUNKS, FEAT])
        dmean = sb("dmean", [P, K])
        prod = sb("prod", [P, N, FEAT, CHUNKS])
        mu = sb("mu", [P, N, 2 * K])
        mu2 = sb("mu2", [P, N, K])
        varw = sb("varw", [P, N, K + 1])
        logs = sb("logs", [P, N, K + 1])
        ivar = sb("ivar", [P, N, K])
        coef = sb("coef", [P, N, 2 * K])
        cdiff = sb("cdiff", [P, 2 * K])
        lterm = sb("lterm", [P, N, K + 1])
        ldiff = sb("ldiff", [P, K + 1])
        lconst = sb("lconst", [P, 1])
        odds = sb("odds", [P, CHUNKS])
        logp = sb("logp", [P, N, CHUNKS])
        esum = sb("esum", [P, CHUNKS])
        resp = sb("resp", [P, N, CHUNKS])
        part = sb("part", [P, N, FEAT])
        rn = sb("rn", [P, N])
        small = sb("small", [P, 8, K])
        xsum = sb("xsum", [P, 2, TILES, 2, S])
        csum = sb("csum", [P, TILES, S])
        cedge = sb("cedge", [P, 4, TILES])
        cmean = sb("cmean", [P, TILES])
        gate = sb("gate", [P, TILES])
        gt = sb("gt", [P, TILES, K])
        chmean = sb("chmean", [P, TILES, 2])
        squeeze = sb("squeeze", [P, 1])
        scale = sb("scale", [P, 2, TILES * 2])
        shift = sb("shift", [P, 2, TILES * 2])
        ps = ctx.enter_context(nc.psum_tensor("ps", [P, 8, 512], F32))

        ident = cst[:, C_ID:C_ID + P]

        passed = sem("passed")
        tables_in = sem("tables_in")
        setup_in = sem("setup_in")
        taps_ready = [sem(f"taps_ready{t}") for t in range(TILES)]
        pads_ready = sem("pads_ready")
        bn_var = sem("bn_var")
        bn_root = sem("bn_root")
        x_in = [sem(f"x_in{h}") for h in range(2)]
        xres_in = [[sem(f"xres_in{h}{i}") for i in range(2)] for h in range(2)]
        stored = [[sem(f"stored{h}{i}") for i in range(2)] for h in range(2)]
        halo = sem("halo")
        conv_ps = sem("conv_ps")
        conv_taken = sem("conv_taken")
        conv_done = sem("conv_done")
        xsummed = sem("xsummed")
        staged = sem("staged")
        tp = [sem(f"tp{i}") for i in range(3)]
        tc = [sem(f"tc{i}") for i in range(3)]
        interp_ready = sem("interp_ready")
        up_ps = [sem(f"up_ps{i}") for i in range(2)]
        up_taken = [sem(f"up_taken{i}") for i in range(2)]
        shifted = [sem(f"shifted{i}") for i in range(2)]
        result = [sem(f"result{i}") for i in range(2)]
        km_x = sem("km_x")
        km_t = [sem(f"km_t{h}") for h in range(2)]
        km_c = [sem(f"km_c{h}") for h in range(2)]
        km_g = [sem(f"km_g{h}") for h in range(2)]
        km_up = sem("km_up")
        km_low = sem("km_low")
        km_dve = sem("km_dve")
        km_pe = sem("km_pe")
        km_done = sem("km_done")
        v_ps = sem("v_ps")
        em_stat = sem("em_stat")
        em_stat_ps = sem("em_stat_ps")
        em_var = sem("em_var")
        em_logs = sem("em_logs")
        em_mix = sem("em_mix")
        em_coef = sem("em_coef")
        em_const = sem("em_const")
        em_logp = sem("em_logp")
        em_exp = sem("em_exp")
        em_part = sem("em_part")
        em_sum = sem("em_sum")
        fin_dve = sem("fin_dve")
        fin_act = sem("fin_act")
        fin_pe = sem("fin_pe")
        params = sem("params")

        TABLE_DMAS, SETUP_DMAS = 2, 5
        xv = x.rearrange("b (t c i) (s r) w -> b t c i s (r w)", t=TILES, i=2, r=XR)
        ov = out.rearrange("b (t c i) (s r) w -> b t c i s (r w)", t=TILES, i=2, r=XR)

        def dram(view, b, t, s):
            return view[ds(b, 1), t, :, :, ds(s, 1), :].rearrange("a c i s f -> c (a i) (s f)")

        def dram_channel(view, b, t, s, i):
            return view[ds(b, 1), t, :, i, ds(s, 1), :].rearrange("a c s f -> c (a s f)")

        def stages(eng, stage_body):
            stage_body(0, 0, True, False, False)
            stage_body(1, 1, True, True, False)
            with eng.Fori(1, B // 2) as jj:
                for p in range(2):
                    stage_body(2 * jj + p, p, True, True, True)
            stage_body(B, 0, False, True, True)
            stage_body(B + 1, 1, False, False, True)

        def runs(em, eng, body):
            if not em:
                for t in range(TILES):
                    with eng.Fori(0, U) as u:
                        body(t, u, "none", 0)
                return
            body(0, 0, "start", 0)
            with eng.Fori(1, U) as u:
                body(0, u, "iterate", 2 * u - 2)
            with eng.Fori(0, 2) as u:
                body(1, u, "iterate", 2 * u + 2 * (U - 1))
            for u in range(2, U):
                body(1, u, "finish", 0)

        free_from_start = {"tensor": [*tp, *up_ps], "scalar": tc,
                           "vector": [conv_taken, *up_taken]}

        def wait_all(eng, *waits):
            waits = [(s_, v if isinstance(v, int) else eng.snap(v)) for s_, v in waits
                     if not (isinstance(v, int) and v == 0)]
            for s_, v in waits:
                eng.wait_ge(s_, v)
            eng.sem_inc(passed)

        def diagonals(eng, t):
            for n, (i, ky, kx) in enumerate(TAPS[:MAX_PE_TAPS]):
                k = 9 * i + 3 * ky + kx
                if eng is nc.scalar:
                    eng.activation(taps[:, t, n, :], ident, ACT.Copy, scale=wd[:, t, k:k + 1])
                else:
                    eng.tensor_scalar(taps[:, t, n, :], ident, wd[:, t, k:k + 1], None, ALU.mult)
            eng.drain().then_inc(taps_ready[t], 1)

        def made_early(j, phase):
            return isinstance(j, int) and j == 1 and phase == "start"

        def conv_sum(do_out, h):
            return ps[:, PS_CONV if do_out or h == 0 else PS_UP, :].rearrange("c (r w) -> c r w", w=WC)

        def tap_input(h, i, ky, kx):
            rows = slice(ky, ky + XR - 1, 2)
            return xin[:, h, i, rows, 1:W - 2:2] if kx == 0 else xin[:, h, i, rows, kx - 1:W:2]

        block = ctx.enter_context(nc.Block())

        @block.sync
        def _(sp):
            sp.dma_start(cst[:, :], consts).then_inc(tables_in, 16)
            sp.dma_start(wd[:, :, :], w_down).then_inc(tables_in, 16)

            def load(b, t, s, h):
                sp.dma_start(xin[:, h, :, 1:XR + 1, :].rearrange("c i r w -> c i (r w)"),
                             dram(xv, b, t, s)).then_inc(x_in[h], 16)

            def load_again(b, t, s, h, i):
                sp.dma_start(xres[:, h, i, :, :].rearrange("c r w -> c (r w)"),
                             dram_channel(xv, b, t, s, i)).then_inc(xres_in[h][i], 16)

            load(0, 0, 0, 0)
            load(0, 0, 1, 1)
            for tile, src in ((wc[:, :, :].rearrange("c k n -> c (k n)"), w_conv), (wu[:, :, :], w_up),
                              (wg[:, :, :], w_guide), (wf[:, :, :], w_fuse), (bnp[:, :, :], bn)):
                sp.dma_start(tile, src).then_inc(setup_in, 16)

            def stage_body(j, do_conv, do_out, more_conv=True, more_out=True):
                def step(t, u, h, nb, nt, nu):
                    g = STEPS * j + S * t + 2 * u + h
                    o = g - 2 * STEPS
                    if do_conv and (nb == 0 or more_conv):
                        wait_all(sp,
                                 (conv_ps, g + 1),
                                 (xsummed, g + 1),
                                 (conv_done, g + 1))
                        wait_all(sp, (halo, g + 2))
                        load(j + nb, nt, 2 * nu + h, h)
                    if do_out:
                        for i in range(2):
                            sp.wait_ge(result[i], o + 1)
                            sp.dma_start(dram_channel(ov, j - 2, t, 2 * u + h, i),
                                         xres[:, h, i, :, :].rearrange("c r w -> c (r w)")) \
                                .then_inc(stored[h][i], 16)
                        if nb == 0 or more_out:
                            for i in range(2):
                                wait_all(sp, (stored[h][i],
                                              16 * (STEPS // 2 * (j - 2) + U * t + u + 1)))
                                load_again(j - 2 + nb, nt, 2 * nu + h, h, i)

                for t in range(TILES):
                    with sp.Fori(0, U - 1) as u:
                        for h in range(2):
                            step(t, u, h, 0, t, u + 1)
                    for h in range(2):
                        step(t, U - 1, h, *((0, t + 1, 0) if t + 1 < TILES else (1, 0, 0)))

            stage_body(0, True, False)
            stage_body(1, True, False)
            sp.wait_ge(km_done, 1)
            for h in range(2):
                for i in range(2):
                    load_again(0, 0, h, h, i)
            with sp.Fori(1, B // 2 - 1) as jj:
                for p in range(2):
                    stage_body(2 * jj + p, True, True)
            stage_body(B - 2, True, True)
            stage_body(B - 1, True, True, more_conv=False)
            stage_body(B, False, True)
            stage_body(B + 1, False, True, more_out=False)
            for h in range(2):
                for i in range(2):
                    sp.wait_ge(stored[h][i], 16 * B * STEPS // 2)

        @block.gpsimd
        def _(pool):
            pool.memset(ones[:, :], 1.0)
            pool.memset(feat[:, :, 2 * K], 1.0)
            pool.memset(stage[:, CR, :], 0.0)
            for p in range(2):
                pool.memset(conv[:, p, TILES * PX:], 0.0)
            pool.drain().then_inc(pads_ready, 1)

            def halo_row(g, h, prev_count):
                wait_all(pool,
                         (conv_done, g - 1),
                         (x_in[1 - h], prev_count))
                pool.tensor_copy(xin[:, h, :, 0, :], xin[:, 1 - h, :, XR, :]).then_inc(halo, 1)

            def halo_zero(g):
                if not (isinstance(g, int) and g == 0):
                    wait_all(pool,
                             (conv_done, g - 1))
                pool.memset(xin[:, 0, :, 0, :], 0.0).then_inc(halo, 1)

            def em_coefficients(e, mix):
                pool.wait_ge(em_mix, mix + 1)
                pool.tensor_tensor(coef[:, :, 0:K], mu[:, :, 0:K], ivar[:, :, :], ALU.mult)
                pool.tensor_scalar(coef[:, :, K:2 * K], ivar[:, :, :], -0.5, None, ALU.mult)
                pool.tensor_tensor(lterm[:, :, 0:K], mu2[:, :, :], ivar[:, :, :], ALU.mult)
                pool.drain()
                pool.tensor_tensor(cdiff[:, :], coef[:, 1, :], coef[:, 0, :], ALU.subtract)
                pool.drain().then_inc(em_coef, 1)
                pool.wait_ge(em_logs, e + 1)
                pool.tensor_tensor(lterm[:, :, 0:K], lterm[:, :, 0:K], logs[:, :, 0:K], ALU.add)
                pool.tensor_scalar(lterm[:, :, K], logs[:, :, K], -2.0, float(K * np.log(2 * np.pi)),
                                   ALU.mult, ALU.add)
                pool.drain()
                pool.tensor_tensor(ldiff[:, :], lterm[:, 0, :], lterm[:, 1, :], ALU.subtract)
                pool.drain()
                width = K
                while width > 1:
                    width //= 2
                    pool.tensor_tensor(ldiff[:, 0:width], ldiff[:, 0:width], ldiff[:, width:2 * width],
                                       ALU.add)
                    pool.drain()
                pool.tensor_tensor(ldiff[:, 0:1], ldiff[:, 0:1], ldiff[:, K:K + 1], ALU.add)
                pool.drain()
                pool.tensor_scalar(lconst[:, :], ldiff[:, 0:1], 0.5, None, ALU.mult)
                pool.drain().then_inc(em_const, 1)

            def stage_body(j, p, do_conv, do_em, do_out):
                def halo_of(t, u, h, top):
                    g = STEPS * j + S * t + 2 * u + h
                    landed = 8 * (STEPS * j + S * t) + 16 * u
                    if top and h == 0:
                        halo_zero(g)
                    else:
                        halo_row(g, h, landed + 16 * h)

                def rows(t, u, h):
                    o = STEPS * (j - 2) + S * t + 2 * u + h
                    wait_all(pool,
                             (tp[2], o + 1))
                    pool.tensor_copy(stage[:, 0, :], stage[:, CR, :])
                    pool.drain()
                    pool.tensor_copy(stage[:, 1:, :],
                                     conv[:, p, ds(t * PX + CN * (2 * u + h), CN + WC)]
                                     .rearrange("c (r w) -> c r w", w=WC)).then_inc(staged, 1)

                def weights(t, u, h):
                    o = STEPS * (j - 2) + S * t + 2 * u + h
                    pool.wait_ge(up_ps[1], o + 1)
                    pool.tensor_tensor(
                        interp[:, :, :],
                        cst[:, ds(C_COEF + XR * (2 * u + h), XR)].unsqueeze(2).to_broadcast([P, XR, W]),
                        cst[:, C_U:C_U + W].unsqueeze(1).to_broadcast([P, XR, W]),
                        ALU.mult).then_inc(interp_ready, 1)

                def round_(t, u, top, em=None):
                    for h in range(2):
                        if do_out:
                            rows(t, u, h)
                        if do_conv:
                            halo_of(t, u, h, top)
                        if em is not None:
                            em_coefficients(EM_ITERS * (j - 1) + em + h, (EM_ITERS + 1) * (j - 1) + em + h)
                        if do_out:
                            weights(t, u, h)

                if do_out:
                    pool.wait_ge(conv_done, STEPS * (j - 1))
                if not do_em:
                    for t in range(TILES):
                        round_(t, 0, True)
                        with pool.Fori(1, U) as u:
                            round_(t, u, False)
                    return
                round_(0, 0, True)
                with pool.Fori(1, U) as u:
                    round_(0, u, False, 2 * u - 2)
                round_(1, 0, True, 2 * (U - 1))
                round_(1, 1, False, 2 * U)
                for u in range(2, U):
                    round_(1, u, False)

            stage_body(0, 0, True, False, False)
            stage_body(1, 1, True, True, False)
            with pool.Fori(1, B // 2) as jj:
                for p in range(2):
                    stage_body(2 * jj + p, p, True, True, True)
            stage_body(B, 0, False, True, True)
            stage_body(B + 1, 1, False, False, True)

        @block.scalar
        def _(act):
            for free in free_from_start["scalar"]:
                act.sem_inc(free)
            act.wait_ge(tables_in, 16 * TABLE_DMAS)
            diagonals(act, 1)

            def k_means():
                def copy_round(q):
                    for h in range(2):
                        act.wait_ge(km_t[h], q + 1)
                        if not (isinstance(q, int) and q == 0):
                            act.wait_ge(km_g[h], q)
                        act.activation(xnormT[:, h, :], ps[:, PS_T + h, 0:TILES * P], ACT.Copy) \
                            .then_inc(km_c[h], 1)
                copy_round(0)
                with act.Fori(1, CHUNKS // 2) as q:
                    copy_round(q)

            def stage_body(j, p, do_conv, do_em, do_out):
                def step(t, u, h, phase, em):
                    g = STEPS * j + S * t + 2 * u + h
                    o = g - 2 * STEPS
                    if do_out:
                        act.wait_ge(up_ps[1], o + 1)
                        act.wait_ge(tp[0], o + 2)
                        act.activation(pairs[:, CR, :], ps[:, PS_CONV, 0:P], ACT.Copy).then_inc(tc[0], 1)
                        for i in range(2):
                            act.wait_ge(tp[1 + i], o + 2)
                            act.activation(pairs[:, 4 * i:4 * i + 4, :].rearrange("c r w -> c (r w)"),
                                           ps[:, PS_T + i, :], ACT.Copy).then_inc(tc[1 + i], 1)
                    if phase == "iterate":
                        e = EM_ITERS * (j - 1) + em + h
                        act.wait_ge(em_var, (EM_ITERS + 1) * (j - 1) + em + h + 1)
                        act.activation(logs[:, :, :], varw[:, :, :], ACT.Ln).then_inc(em_logs, 1)
                        act.wait_ge(em_logp, e + 1)
                        for n in range(N):
                            r = act.activation(resp[:, n, :], logp[:, n, :], ACT.Exp,
                                               scale=-1.0 if n == 0 else 1.0)
                        r.then_inc(em_exp, 1)
                    if phase == "finish" and (u, h) == (2, 0):
                        act.wait_ge(fin_dve, 3 * (j - 1) + 1)
                        act.activation(small[:, 3, :], small[:, 2, :], ACT.Exp, scale=-1.0) \
                            .then_inc(fin_act, 1)
                    if do_out:
                        for i in range(2):
                            act.wait_ge(xres_in[h][i], 8 * (STEPS * (j - 2) + S * t) + 16 * u + 16)
                            c = xres[:, h, i, :, :].rearrange("c r w -> c (r w)")
                            act.activation(c, c, ACT.Identity, bias=shift[:, p, 2 * t + i:2 * t + i + 1]) \
                                .then_inc(shifted[i], 1)
                    if do_conv:
                        act.wait_ge(x_in[h], 8 * (STEPS * j + S * t) + 16 * u + 16)
                        for i in range(2):
                            act.activation(junk[:, :], xin[:, h, i, 1:, :].rearrange("c r w -> c (r w)"),
                                           ACT.Copy, accum_out=xsum[:, p, t, i, ds(2 * u + h, 1)])
                            d = act.drain()
                        d.then_inc(xsummed, 1)
                    if do_em and t == 0:
                        if phase == "start" and h == 0:
                            act.wait_ge(conv_done, STEPS * j)
                        for tile in range(TILES):
                            act.activation(junk[:, 0:CN],
                                           conv[:, 1 - p, ds(tile * PX + CN * (2 * u + h), CN)],
                                           ACT.Copy, accum_out=csum[:, tile, ds(2 * u + h, 1)])
                            act.drain()

                def round_(t, u, phase, em):
                    for h in range(2):
                        step(t, u, h, phase, em)

                if do_out:
                    act.wait_ge(params, j - 1)
                runs(do_em, act, round_)

            stage_body(0, 0, True, False, False)
            act.wait_ge(bn_var, 1)
            act.activation(inv_std[:, :], inv_std[:, :], ACT.Sqrt).then_inc(bn_root, 1)
            act.preload_act_table_set("natural_log_exp_and_others")
            k_means()
            stage_body(1, 1, True, True, False)
            with act.Fori(1, B // 2) as jj:
                for p in range(2):
                    stage_body(2 * jj + p, p, True, True, True)
            stage_body(B, 0, False, True, True)
            stage_body(B + 1, 1, False, False, True)

        @block.tensor
        def _(pe):
            for free in free_from_start["tensor"]:
                pe.sem_inc(free)

            def conv_taps(j, t, u, h, phase, do_out):
                g = STEPS * j + S * t + 2 * u + h
                o = g - 2 * STEPS
                pe.wait_ge(x_in[h], 8 * (STEPS * j + S * t) + 16 * u + 16)
                pe.wait_ge(conv_taken, g + 2 if do_out else g + 1)
                if do_out:
                    pe.wait_ge(tc[0], o + 2)
                acc = conv_sum(do_out, h)
                if isinstance(j, int) and j == 0:
                    pe.wait_ge(taps_ready[t], 1)
                mine = tap_shares(j, phase)[0]
                for n, (i, ky, kx) in enumerate(mine):
                    last = n == len(mine) - 1
                    if ky == 0 and TAPS[n - 1][1] != 0:
                        pe.wait_ge(halo, g + 1)
                    mm = pe.matmul(acc[:, :, 1:] if kx == 0 else acc, taps[:, t, n, :],
                                   tap_input(h, i, ky, kx), start=n == 0, stop=last)
                mm.then_inc(conv_ps, 1)

            def means(bank, p, weights, blocks):
                per = CN // P
                for c in range(per * blocks[0], per * blocks[1]):
                    for t in range(TILES):
                        m = pe.matmul(ps[:, bank, c * K:(c + 1) * K],
                                      conv[:, p, t * PX + c * P:t * PX + (c + 1) * P],
                                      weights[:, t, :], start=t == 0, stop=t == TILES - 1)
                return m

            def k_means():
                def turn(q, h, first=False):
                    pe.wait_ge(km_x, 2 * q + h + 1)
                    if not first:
                        pe.wait_ge(km_c[h], q)
                    for t in range(TILES):
                        m = pe.transpose(ps[:, PS_T + h, t * P:(t + 1) * P], xnorm[:, h, t, :], ident)
                    m.then_inc(km_t[h], 1)

                def gram_product(q, h, first=False, last=False):
                    pe.wait_ge(km_c[h], q + 1)
                    for a in range(TILES):
                        m = pe.matmul(ps[:, PS_GRAM + a, a * P:TILES * P], xnormT[:, h, a * P:(a + 1) * P],
                                      xnormT[:, h, a * P:], start=first, stop=last)
                    m.then_inc(km_g[h], 1)

                ROUNDS = CHUNKS // 2
                for h in range(2):
                    conv_taps(1, 0, 0, h, "start", False)
                turn(0, 0, first=True)
                turn(0, 1, first=True)
                gram_product(0, 0, first=True)
                turn(1, 0)
                gram_product(0, 1)
                with pe.Fori(1, ROUNDS - 1) as q:
                    turn(q, 1)
                    gram_product(q, 0)
                    turn(q + 1, 0)
                    gram_product(q, 1)
                turn(ROUNDS - 1, 1)
                gram_product(ROUNDS - 1, 0)
                gram_product(ROUNDS - 1, 1, last=True)
                pe.wait_ge(km_up, 1)
                pe.transpose(ps[:, PS_GRAM + 2, 0:P], gram[:, 0, P:2 * P], ident).then_inc(km_low, 1)

                def over_channels(bank, col, weights, values):
                    for t in range(TILES):
                        m = pe.matmul(ps[:, bank, col:col + K], weights(t), values[:, t, :],
                                      start=t == 0, stop=t == TILES - 1)
                    return m

                def all_ones(t):
                    return ones[:, :]

                with pe.Fori(0, KM_ITERS + 1) as it:
                    pe.wait_ge(km_dve, 2 * it + 1)
                    for a in range(TILES):
                        m = over_channels(PS_SMALL, K * a, lambda t: gram[:, t, a * P:(a + 1) * P], member)
                    m.then_inc(km_pe, 1)
                    over_channels(PS_T + 1, 0, all_ones, member).then_inc(km_pe, 1)
                    pe.wait_ge(km_dve, 2 * it + 2)
                    over_channels(PS_T, 0, all_ones, kt).then_inc(km_pe, 1)
                n = 2 * (KM_ITERS + 1)
                pe.wait_ge(km_dve, n + 1)
                over_channels(PS_SMALL, 0, all_ones, member).then_inc(km_pe, 1)
                pe.wait_ge(km_dve, n + 2)
                means(PS_T + 1, 0, member_n, (0, S)).then_inc(km_pe, 1)
                for i in range(2):
                    pe.wait_ge(km_dve, n + 3 + i)
                    pe.matmul(ps[:, PS_SMALL, 0:K], ones[:, :], part[:, 0, 0:K], start=True, stop=True) \
                        .then_inc(km_pe, 1)

            def next_means(j, p, u, h):
                if (u, h) == (2, 0):
                    pe.wait_ge(km_done, 1)
                    pe.wait_ge(fin_dve, 3 * (j - 1) + 1)
                elif (u, h) == (3, 0):
                    pe.wait_ge(fin_dve, 3 * (j - 1) + 3)
                elif (u, h) == (3, 1):
                    pe.wait_ge(params, j)
                blocks = {(2, 0): (0, 2), (2, 1): (2, 4), (3, 0): (4, 6), (3, 1): (6, S - 1)}[u, h]
                pe.wait_ge(conv_done, STEPS * j + S + blocks[1])
                means(PS_SMALL, p, mean_w, blocks)

            def mixture_mean(b):
                pe.wait_ge(em_stat, 2 * b + 1)
                pe.matmul(ps[:, PS_SMALL, SM_SUM:SM_SUM + K], ones[:, :], part[:, 0, 0:K],
                          start=True, stop=True).then_inc(em_stat_ps, 1)

            def mixture_start(b):
                pe.wait_ge(em_stat, 2 * b + 2)
                for n, (weights, values) in enumerate((
                        (cst[:, C_FIRST:C_FIRST + P], feat[:, 0, 0:K]),
                        (cst[:, C_LAST:C_LAST + P], feat[:, CHUNKS - 1, 0:K]),
                        (ones[:, :], part[:, 0, 0:K]))):
                    m = pe.matmul(ps[:, PS_SMALL, SM_SUM + n * K:SM_SUM + (n + 1) * K], weights, values,
                                  start=True, stop=True)
                m.then_inc(em_stat_ps, 1)

            def excite_in(b):
                pe.wait_ge(fin_dve, 3 * b + 2)
                for n in range(2 * TILES):
                    m = pe.matmul(ps[:, PS_SMALL, SM_Y1:SM_Y1 + 1], wg[:, n, :],
                                  chmean[:, :, :].rearrange("c t i -> c (t i)")[:, n:n + 1],
                                  start=n == 0, stop=n == 2 * TILES - 1)
                m.then_inc(fin_pe, 1)

            def excite_out(b):
                pe.wait_ge(fin_dve, 3 * b + 3)
                for n in range(2 * TILES):
                    m = pe.matmul(ps[:, PS_SMALL, SM_Y2 + n:SM_Y2 + n + 1], wf[:, n, :],
                                  squeeze[:, :], start=True, stop=True)
                m.then_inc(fin_pe, 1)

            def stage_body(j, p, do_conv, do_em, do_out):
                def step(t, u, h, phase, em):
                    g = STEPS * j + S * t + 2 * u + h
                    o = g - 2 * STEPS
                    if do_out:
                        pe.wait_ge(staged, o + 1)
                        pe.wait_ge(conv_taken, g + 2 if do_conv else B * STEPS + 2)
                        pe.transpose(ps[:, PS_CONV, 0:P],
                                     stage[:, CR:CR + 2, :].rearrange("c r w -> c (r w)"), ident) \
                            .then_inc(tp[0], 1)
                        for i in range(2):
                            pe.wait_ge(tc[1 + i], o + 1)
                            for m in range(4):
                                k = 4 * i + m
                                mm = pe.transpose(ps[:, PS_T + i, m * P:(m + 1) * P],
                                                  stage[:, k:k + 2, :].rearrange("c r w -> c (r w)"), ident)
                            mm.then_inc(tp[1 + i], 1)
                    if phase == "start" and h == 1:
                        mixture_mean(j - 1)
                    if do_conv and not made_early(j, phase):
                        conv_taps(j, t, u, h, phase, do_out)
                    if phase == "start":
                        if h == 0:
                            if not (isinstance(j, int) and j == 1):
                                pe.wait_ge(conv_done, STEPS * j)
                                means(PS_SMALL, 1 - p, mean_w, (S - 1, S)).then_inc(v_ps, 1)
                        else:
                            mixture_start(j - 1)
                    if phase == "finish":
                        if do_conv:
                            next_means(j, p, u, h)
                        if (u, h) == (2, 1):
                            excite_in(j - 1)
                        elif (u, h) == (3, 0):
                            excite_out(j - 1)
                    def mixture_sums():
                        e = EM_ITERS * (j - 1) + em + h
                        pe.wait_ge(em_part, e + 1)
                        pe.matmul(ps[:, PS_SMALL, SM_SUM:SM_SUM + N * FEAT], ones[:, :],
                                  part[:, :, :].rearrange("c n k -> c (n k)"),
                                  start=True, stop=True).then_inc(em_sum, 1)

                    if phase == "iterate" and do_conv:
                        mixture_sums()
                    if do_out:
                        pe.wait_ge(interp_ready, o + 1)
                        for i in range(3):
                            pe.wait_ge(tc[i], o + 2)
                        for half, ms in ((0, (1, 2, 3, 4)), (1, (5, 6, 7, 8, 0))):
                            pe.wait_ge(up_taken[half], o + 1)
                            for m in ms:
                                pos, n = (2 * m - 2, 2) if 0 < m < CR else (2 * CR - 2, 1) if m else (2 * CR - 1, 1)
                                mm = pe.matmul(ps[:, PS_UP + pos // 4, (pos % 4) * W:(pos % 4 + n) * W],
                                               pairs[:, m, :],
                                               interp[:, pos:pos + n, :].rearrange("c r w -> c (r w)"),
                                               start=True, stop=True)
                            mm.then_inc(up_ps[half], 1)
                    if phase == "iterate" and not do_conv:
                        mixture_sums()

                def round_(t, u, phase, em):
                    for h in range(2):
                        step(t, u, h, phase, em)

                runs(do_em, pe, round_)

            stage_body(0, 0, True, False, False)
            pe.wait_ge(pads_ready, 1)
            k_means()
            stage_body(1, 1, True, True, False)
            with pe.Fori(1, B // 2) as jj:
                for p in range(2):
                    stage_body(2 * jj + p, p, True, True, True)
            stage_body(B, 0, False, True, True)
            stage_body(B + 1, 1, False, False, True)

        @block.vector
        def _(dve):
            def tt(out_, a, b, op):
                dve.tensor_tensor(out_, a, b, op)
                return dve.drain()

            def tsc(out_, a, s1, s2, op0, op1=ALU.bypass):
                dve.tensor_scalar(out_, a, s1, s2, op0, op1) if s2 is not None else \
                    dve.tensor_scalar(out_, a, s1, None, op0)
                return dve.drain()

            def stt(out_, a, s, b, op0, op1):
                dve.scalar_tensor_tensor(out_, a, s, b, op0, op1)
                return dve.drain()

            def red(out_, a, op=ALU.add):
                dve.tensor_reduce(out_, a, AX.X, op)
                return dve.drain()

            def recip(out_, a):
                dve.reciprocal(out_, a)
                return dve.drain()

            for free in free_from_start["vector"]:
                dve.sem_inc(free)
            dve.sem_inc(conv_taken)
            dve.wait_ge(tables_in, 16 * TABLE_DMAS)
            diagonals(dve, 0)

            f_ck = feat[:, :, :]
            f_kc = feat[:, :, :].rearrange("p c k -> p k c")

            def conv_taps(j, p, t, u, h, phase, em, do_out):
                g = STEPS * j + S * t + 2 * u + h
                o = g - 2 * STEPS
                dve.wait_ge(x_in[h], 8 * (STEPS * j + S * t) + 16 * u + 16)
                rows = conv[:, p, ds(t * PX + CN * (2 * u + h), CN)].rearrange(
                    "c (r w) -> c r w", w=WC)
                acc = conv_sum(do_out, h)
                if do_out:
                    dve.wait_ge(staged, o + 1)
                    dve.wait_ge(conv_ps, g + 1)
                dve.wait_ge(halo, g + 1)
                for n, (i, ky, kx) in enumerate(tap_shares(j, phase)[1]):
                    k = 9 * i + 3 * ky + kx
                    src = tap_input(h, i, ky, kx)
                    to = rows[:, :, 1:] if kx == 0 else rows
                    if n > 0:
                        dve.scalar_tensor_tensor(to, src, wd[:, t, k:k + 1], to, ALU.mult, ALU.add)
                        d = dve.drain()
                    elif do_out:
                        dve.scalar_tensor_tensor(to, src, wd[:, t, k:k + 1], acc, ALU.mult, ALU.add)
                        dve.drain().then_inc(conv_taken, 1)
                    else:
                        dve.tensor_scalar(to, src, wd[:, t, k:k + 1], None, ALU.mult)
                        dve.drain()
                if not do_out:
                    if phase == "iterate":
                        em_update(EM_ITERS * (j - 1) + em + h)
                    dve.wait_ge(conv_ps, g + 1)
                    dve.tensor_tensor(rows, rows, acc, ALU.add)
                    dve.drain().then_inc(conv_taken, 1)
                    d = dve.drain()
                d.then_inc(conv_done, 1)

            def k_means():
                both = conv[:, 0, 0:TILES * PX].rearrange("c (t x) -> c t x", t=TILES)
                dve.tensor_reduce(lo[:, :], both, AX.X, ALU.min)
                red(hi[:, :], both, ALU.max)
                tt(hi[:, :], hi[:, :], lo[:, :], ALU.subtract)
                tsc(hi[:, :], hi[:, :], 1e-12, None, ALU.max)
                recip(hi[:, :], hi[:, :])

                def normalise(q):
                    for h in range(2):
                        if not (isinstance(q, int) and q == 0):
                            dve.wait_ge(km_t[h], q)
                        for t in range(TILES):
                            m = dve.tensor_scalar(xnorm[:, h, t, :],
                                                  conv[:, 0, ds(t * PX + P * (2 * q + h), P)],
                                                  lo[:, t:t + 1], hi[:, t:t + 1], ALU.subtract, ALU.mult)
                        m.then_inc(km_x, 1)
                normalise(0)
                with dve.Fori(1, CHUNKS // 2) as q:
                    normalise(q)

                dve.wait_ge(km_g[1], CHUNKS // 2)
                for a in range(TILES):
                    dve.tensor_copy(gram[:, a, a * P:], ps[:, PS_GRAM + a, a * P:TILES * P])
                dve.drain().then_inc(km_up, 1)
                for a in range(TILES):
                    tt(gdiag[:, :], gram[:, a, a * P:(a + 1) * P], ident, ALU.mult)
                    red(sq[:, a:a + 1], gdiag[:, :])
                dve.wait_ge(km_low, 1)
                dve.tensor_copy(gram[:, 1, 0:P], ps[:, PS_GRAM + 2, 0:P])
                dve.memset(dots[:, :, :], 0.0)
                dve.memset(c2[:, 0, :], 0.0)
                dve.tensor_copy(member[:, :, :].rearrange("c t k -> c (t k)"),
                                cst[:, C_SEED:C_SEED + TILES * K])
                dve.drain().then_inc(km_dve, 1)

                def wide(v, shape=(P, TILES, K)):
                    return v.unsqueeze(1 if v.shape[1] == K else 2).to_broadcast(list(shape))

                prefer = cst[:, C_PREF:C_PREF + K]
                dve.tensor_copy(point_sq[:, :, :], wide(sq[:, :]))
                dve.drain()
                def flat_(t_):
                    return t_[:, :, :].rearrange("c t k -> c (t k)")

                with dve.Fori(0, KM_ITERS + 1) as it:
                    dve.wait_ge(km_pe, 3 * it + 1)
                    products = ps[:, PS_SMALL, 0:TILES * K]
                    count = ps[:, PS_T + 1, 0:K]
                    tt(flat_(kt), products, flat_(member), ALU.mult).then_inc(km_dve, 1)
                    dve.wait_ge(km_pe, 3 * it + 2)
                    dve.tensor_scalar(cnt[:, 0, :], count, 1.0, None, ALU.max)
                    tsc(cnt[:, 2, :], count, 0.0, None, ALU.is_le)
                    recip(cnt[:, 1, :], cnt[:, 0, :])
                    dve.tensor_tensor(dots[:, :, :], dots[:, :, :], wide(cnt[:, 2, :]), ALU.mult)
                    dve.tensor_tensor(c2[:, 0, :], c2[:, 0, :], cnt[:, 2, :], ALU.mult)
                    dve.tensor_tensor(cnt[:, 0, :], cnt[:, 1, :], cnt[:, 1, :], ALU.mult)
                    tt(dist[:, :, :], products.rearrange("c (t k) -> c t k", t=TILES), wide(cnt[:, 1, :]),
                       ALU.mult)
                    tt(dots[:, :, :], dots[:, :, :], dist[:, :, :], ALU.add)
                    stt(flat_(dist), flat_(dots), -2.0, flat_(point_sq), ALU.mult, ALU.add)
                    dve.wait_ge(km_pe, 3 * it + 3)
                    tt(c2[:, 1, :], ps[:, PS_T, 0:K], cnt[:, 0, :], ALU.mult)
                    tt(c2[:, 0, :], c2[:, 0, :], c2[:, 1, :], ALU.add)
                    tt(dist[:, :, :], dist[:, :, :], wide(c2[:, 0, :]), ALU.add)
                    red(kbest[:, :], dist[:, :, :], ALU.min)
                    tt(dist[:, :, :], dist[:, :, :], wide(kbest[:, :]), ALU.is_equal)
                    tt(dist[:, :, :], dist[:, :, :], wide(prefer), ALU.mult)
                    red(kbest[:, :], dist[:, :, :], ALU.max)
                    tt(member[:, :, :], dist[:, :, :], wide(kbest[:, :]), ALU.is_equal) \
                        .then_inc(km_dve, 1)
                n = 3 * (KM_ITERS + 1)
                dve.wait_ge(km_pe, n + 1)
                tsc(cnt[:, 0, :], ps[:, PS_SMALL, 0:K], 1.0, None, ALU.max)
                recip(cnt[:, 1, :], cnt[:, 0, :])
                tt(member_n[:, :, :], member[:, :, :], wide(cnt[:, 1, :]), ALU.mult).then_inc(km_dve, 1)
                for h in range(2):
                    conv_taps(1, 1, 0, 0, h, "start", 0, False)
                dve.wait_ge(km_pe, n + 2)
                got = ps[:, PS_T + 1, 0:CHUNKS * K].rearrange("p (c k) -> p c k", k=K)
                dve.tensor_copy(kpx[:, :, :], got)
                dve.tensor_reduce(part[:, 0, 0:K], got.rearrange("p c k -> p k c"), AX.X, ALU.add)
                dve.drain().then_inc(km_dve, 1)
                dve.wait_ge(km_pe, n + 3)
                tsc(kv[:, :], ps[:, PS_SMALL, 0:K], 1.0 / PX, None, ALU.mult)
                dev = f_ck[:, :, 0:K]
                tt(dev, kpx[:, :, :], kv[:, :].unsqueeze(1).to_broadcast([P, CHUNKS, K]), ALU.subtract)
                tt(dev, dev, dev, ALU.mult)
                red(part[:, 0, 0:K], f_kc[:, 0:K, :]).then_inc(km_dve, 1)
                dve.wait_ge(km_pe, n + 4)
                dve.tensor_copy(kv[:, :], ps[:, PS_SMALL, 0:K])
                dve.drain()
                other = kv[:, :].unsqueeze(1).to_broadcast([P, K, K])
                own = kv[:, :].unsqueeze(2).to_broadcast([P, K, K])
                tt(klt[:, :, :], other, own, ALU.is_lt)
                tt(keq[:, :, :], other, own, ALU.is_equal)
                tt(keq[:, :, :], keq[:, :, :], cst[:, C_TRI:C_TRI + K * K].rearrange("c (k m) -> c k m", k=K),
                   ALU.mult)
                tt(klt[:, :, :], klt[:, :, :], keq[:, :, :], ALU.add)
                red(rank[:, :], klt[:, :, :])
                tt(kt[:, :, :], member[:, :, :], wide(rank[:, :]), ALU.mult)
                red(kbest[:, :], kt[:, :, :])
                tt(sorted_member[:, :, :], wide(kbest[:, :]), wide(cst[:, C_IOTA:C_IOTA + K]), ALU.is_equal)
                red(kbest[:, :], member_n[:, :, :])
                tt(mean_w[:, :, :], sorted_member[:, :, :], wide(kbest[:, :]), ALU.mult).then_inc(km_done, 1)

            def mixture_mean(b):
                if isinstance(b, int) and b == 0:
                    perm, terms = klt[:, :, :], interp[:, :, :].rearrange("p r w -> p (r w)") \
                        .rearrange("p (c k m) -> p c k m", k=K, m=K)
                    tt(perm, rank[:, :].unsqueeze(1).to_broadcast([P, K, K]),
                       cst[:, C_IOTA:C_IOTA + K].unsqueeze(2).to_broadcast([P, K, K]), ALU.is_equal)
                    tt(terms, kpx[:, :, :].unsqueeze(2).to_broadcast([P, CHUNKS, K, K]),
                       perm.unsqueeze(1).to_broadcast([P, CHUNKS, K, K]), ALU.mult)
                    red(f_ck[:, :, 0:K], terms)
                    got = f_ck[:, :, 0:K]
                else:
                    dve.wait_ge(v_ps, b)
                    got = ps[:, PS_SMALL, 0:CHUNKS * K].rearrange("p (c k) -> p c k", k=K)
                    dve.tensor_copy(f_ck[:, :, 0:K], got)
                dve.tensor_reduce(part[:, 0, 0:K], got.rearrange("p c k -> p k c"), AX.X, ALU.add)
                dve.drain().then_inc(em_stat, 1)

            def mixture_variance():
                tsc(dmean[:, :], ps[:, PS_SMALL, SM_SUM:SM_SUM + K], 1.0 / PX, None, ALU.mult)
                d = f_ck[:, :, 0:K]
                tt(d, d, dmean[:, :].unsqueeze(1).to_broadcast([P, CHUNKS, K]), ALU.subtract)
                tt(f_ck[:, :, K:2 * K], d, d, ALU.mult)
                red(part[:, 0, 0:K], f_kc[:, K:2 * K, :]).then_inc(em_stat, 1)

            def mixture_start():
                dve.tensor_copy(mu[:, :, 0:K], ps[:, PS_SMALL, SM_SUM:SM_SUM + N * K]
                                .rearrange("p (n k) -> p n k", n=N))
                for n in range(N):
                    dve.tensor_scalar(varw[:, n, 0:K], ps[:, PS_SMALL, SM_SUM + N * K:SM_SUM + (N + 1) * K],
                                      1.0 / PX, EPS, ALU.mult, ALU.add)
                    dve.memset(varw[:, n, K:K + 1], 1.0 / N)
                dve.drain()
                tt(mu2[:, :, :], mu[:, :, 0:K], mu[:, :, 0:K], ALU.mult).then_inc(em_var, 1)
                recip(ivar[:, :, :], varw[:, :, 0:K]).then_inc(em_mix, 1)

            def em_update(e):
                dve.wait_ge(em_sum, e + 1)
                sums = ps[:, PS_SMALL, SM_SUM:SM_SUM + N * FEAT].rearrange("p (n k) -> p n k", n=N)
                dve.tensor_scalar(varw[:, :, K], sums[:, :, 2 * K], 1.0 / PX, None, ALU.mult)
                recip(rn[:, :], sums[:, :, 2 * K])
                tt(mu[:, :, :], sums[:, :, 0:2 * K], rn[:, :].unsqueeze(2).to_broadcast([P, N, 2 * K]),
                   ALU.mult)
                tt(mu2[:, :, :], mu[:, :, 0:K], mu[:, :, 0:K], ALU.mult)
                tt(varw[:, :, 0:K], mu[:, :, K:2 * K], mu2[:, :, :], ALU.subtract)
                tsc(varw[:, :, 0:K], varw[:, :, 0:K], EPS, EPS, ALU.add, ALU.max).then_inc(em_var, 1)
                recip(ivar[:, :, :], varw[:, :, 0:K]).then_inc(em_mix, 1)

            def em_expect(e):
                dve.wait_ge(em_coef, e + 1)
                terms = prod[:, 0, :, :].rearrange("p f c -> p (f c)")[:, 0:CHUNKS * 2 * K] \
                    .rearrange("p (c f) -> p c f", f=2 * K)
                tt(terms, f_ck[:, :, 0:2 * K], cdiff[:, :].unsqueeze(1).to_broadcast([P, CHUNKS, 2 * K]),
                   ALU.mult)
                red(odds[:, :], terms)
                dve.wait_ge(em_const, e + 1)
                dve.tensor_scalar(logp[:, 0, :], odds[:, :], lconst[:, 0:1], 0.0, ALU.add, ALU.max)
                dve.tensor_scalar(logp[:, 1, :], odds[:, :], lconst[:, 0:1], 0.0, ALU.add, ALU.min)
                dve.drain().then_inc(em_logp, 1)

            def em_sums(e):
                dve.wait_ge(em_exp, e + 1)
                tt(esum[:, :], resp[:, 0, :], resp[:, 1, :], ALU.add)
                recip(esum[:, :], esum[:, :])
                tt(resp[:, :, :], resp[:, :, :], esum[:, :].unsqueeze(1).to_broadcast([P, N, CHUNKS]),
                   ALU.mult)
                for n in range(N):
                    dve.tensor_tensor(prod[:, n, :, :], f_kc,
                                      resp[:, n, :].unsqueeze(1).to_broadcast([P, FEAT, CHUNKS]), ALU.mult)
                dve.drain()
                red(part[:, :, :], prod[:, :, :, :]).then_inc(em_part, 1)

            def conv_edges(q):
                rows = conv[:, q, 0:TILES * PX].rearrange("c (t h w) -> c t h w", t=TILES, w=WC)
                cols = conv[:, q, 0:TILES * PX].rearrange("c (t h w) -> c t w h", t=TILES, w=WC)
                dve.tensor_reduce(cedge[:, 0, :], rows[:, :, 0:HC:HC - 1, :], AX.XY, ALU.add)
                dve.tensor_reduce(cedge[:, 1, :], cols[:, :, 0:WC:WC - 1, :], AX.XY, ALU.add)
                dve.tensor_reduce(cedge[:, 2, :], rows[:, :, 0:HC:HC - 1, 0:WC:WC - 1], AX.XY, ALU.add)
                dve.drain()
                tt(cedge[:, 0, :], cedge[:, 0, :], cedge[:, 1, :], ALU.add)
                stt(cedge[:, 0, :], cedge[:, 2, :], -0.25, cedge[:, 0, :], ALU.mult, ALU.add)

            def order_components():
                le, gt_, z, s0, s1 = (small[:, i, :] for i in (0, 1, 2, 4, 5))
                dve.tensor_tensor(mu[:, :, 0:K], mu[:, :, 0:K],
                                  dmean[:, :].unsqueeze(1).to_broadcast([P, N, K]), ALU.add)
                tt(le, varw[:, 0, 0:K], varw[:, 1, 0:K], ALU.is_le)
                tsc(gt_, le, -1.0, 1.0, ALU.mult, ALU.add)
                for n, first, second in ((0, le, gt_), (1, gt_, le)):
                    dve.tensor_tensor(s0, first, mu[:, 0, 0:K], ALU.mult)
                    tt(s1, second, mu[:, 1, 0:K], ALU.mult)
                    tt(s0, s0, s1, ALU.add)
                    if n == 0:
                        tt(z, s0, wc[:, :, n], ALU.mult)
                    else:
                        tt(s0, s0, wc[:, :, n], ALU.mult)
                        tt(z, z, s0, ALU.add).then_inc(fin_dve, 1)

            def gate_and_means(q):
                s0 = small[:, 4, :]
                tsc(s0, small[:, 3, :], 1.0, None, ALU.add)
                recip(s0, s0)
                tt(gt[:, :, :], sorted_member[:, :, :], s0.unsqueeze(1).to_broadcast([P, TILES, K]), ALU.mult)
                dve.tensor_reduce(gate[:, :], gt[:, :, :], AX.X, ALU.add)
                dve.tensor_reduce(cmean[:, :], csum[:, :, :], AX.X, ALU.add)
                dve.tensor_reduce(chmean[:, :, :].rearrange("c t i -> c (t i)"),
                                  xsum[:, q, :, :, :].rearrange("c t i s -> c (t i) s"), AX.X, ALU.add)
                dve.drain()
                stt(cmean[:, :], cedge[:, 0, :], -0.25, cmean[:, :], ALU.mult, ALU.add)
                dve.tensor_scalar(cmean[:, :], cmean[:, :], UP * UP, None, ALU.mult)
                tsc(gate[:, :], gate[:, :], 1.0, None, ALU.add)
                new = scale[:, q, :].rearrange("c (t i) -> c t i", t=TILES)
                tt(new, wu[:, :, :], gate[:, :].unsqueeze(2).to_broadcast([P, TILES, 2]), ALU.mult)
                tt(gt[:, :, 0:2], new, cmean[:, :].unsqueeze(2).to_broadcast([P, TILES, 2]), ALU.mult)
                tt(chmean[:, :, :], chmean[:, :, :], gt[:, :, 0:2], ALU.add)
                tsc(chmean[:, :, :], chmean[:, :, :], 1.0 / (H * W), None, ALU.mult).then_inc(fin_dve, 1)

            def excite(q):
                y = small[:, 6, 0:2 * TILES]
                tt(y, ps[:, PS_SMALL, SM_Y2:SM_Y2 + 2 * TILES], bnp[:, 2, :], ALU.subtract)
                tt(y, y, inv_std[:, :], ALU.mult)
                tt(y, y, bnp[:, 0, :], ALU.mult)
                tt(y, y, bnp[:, 1, :], ALU.add)
                tsc(shift[:, q, :], y, 0.0, 6.0, ALU.max, ALU.min).then_inc(params, 1)

            def before_taps(b, q, u, h, phase, em):
                if phase == "start" and h == 1:
                    dve.wait_ge(em_stat_ps, 2 * b + 1)
                    mixture_variance()
                elif phase == "finish" and (u, h) == (2, 0):
                    order_components()
                    conv_edges(q)
                elif phase == "iterate":
                    em_expect(EM_ITERS * b + em + h)
                    em_sums(EM_ITERS * b + em + h)

            def after_taps(b, q, u, h, phase, em):
                if phase == "start":
                    if h == 0:
                        mixture_mean(b)
                    else:
                        dve.wait_ge(em_stat_ps, 2 * b + 2)
                        mixture_start()
                elif phase == "finish":
                    if (u, h) == (2, 0):
                        dve.wait_ge(fin_act, b + 1)
                        gate_and_means(q)
                    elif (u, h) == (2, 1):
                        dve.wait_ge(fin_pe, 2 * b + 1)
                        tsc(squeeze[:, :], ps[:, PS_SMALL, SM_Y1:SM_Y1 + 1], 0.0, 6.0, ALU.max, ALU.min) \
                            .then_inc(fin_dve, 1)
                    elif (u, h) == (3, 0):
                        dve.wait_ge(fin_pe, 2 * b + 2)
                        excite(q)
                elif phase == "iterate":
                    em_update(EM_ITERS * b + em + h)
            def stage_body(j, p, do_conv, do_em, do_out):
                def step(t, u, h, phase, em):
                    g = STEPS * j + S * t + 2 * u + h
                    o = g - 2 * STEPS
                    before_taps(j - 1, 1 - p, u, h, phase, em)
                    if do_conv and not made_early(j, phase):
                        conv_taps(j, p, t, u, h, phase, em, do_out)
                    if do_out or phase != "iterate":
                        after_taps(j - 1, 1 - p, u, h, phase, em)
                    if do_out:
                        for i in range(2):
                            dve.wait_ge(shifted[i], o + 1)
                            for half in range(2):
                                if i == 0:
                                    dve.wait_ge(up_ps[half], o + 2)
                                sc = scale[:, p, 2 * t + i:2 * t + i + 1]
                                up = ps[:, PS_UP:PS_UP + 4, :].rearrange("c b n -> c (b n)")
                                spans = [(1, 9, 0)] if half == 0 else [(9, XR, CR), (0, 1, XR - 1)]
                                for r0, r1, pos in spans:
                                    dst = xres[:, h, i, r0:r1, :].rearrange("c r w -> c (r w)")
                                    m = dve.scalar_tensor_tensor(dst, up[:, pos * W:(pos + r1 - r0) * W],
                                                                 sc, dst, ALU.mult, ALU.add)
                                if i == 1:
                                    m.then_inc(up_taken[half], 1)
                            dve.drain().then_inc(result[i], 1)

                def round_(t, u, phase, em):
                    for h in range(2):
                        step(t, u, h, phase, em)

                runs(do_em, dve, round_)

            stage_body(0, 0, True, False, False)
            dve.wait_ge(pads_ready, 1)
            dve.wait_ge(setup_in, 16 * SETUP_DMAS)
            tsc(inv_std[:, :], bnp[:, 3, :], BN_EPS, None, ALU.add).then_inc(bn_var, 1)
            k_means()
            dve.wait_ge(bn_root, 1)
            recip(inv_std[:, :], inv_std[:, :])
            stage_body(1, 1, True, True, False)
            with dve.Fori(1, B // 2) as jj:
                for p in range(2):
                    stage_body(2 * jj + p, p, True, True, True)
            stage_body(B, 0, False, True, True)
            stage_body(B + 1, 1, False, False, True)


def kernel(x, L0_conv_w_down, L0_conv_w_conv, L0_conv_w_up, L1_conv_w_guide, L1_conv_w_fuse,
           L1_conv_bn_gamma, L1_conv_bn_beta, L1_conv_bn_mean, L1_conv_bn_var):
    import concourse.bacc as bacc
    from concourse.bass_utils import run_bass_kernel_spmd

    def by_channel(v):
        v = np.asarray(v)
        v = v.reshape(TILES, P, 2, *v.shape[1:])
        return np.ascontiguousarray(np.moveaxis(v, 0, 1).reshape(P, TILES * 2, *v.shape[3:]))

    w_down = np.asarray(L0_conv_w_down).reshape(TILES, P, 18).transpose(1, 0, 2)
    w_conv = np.broadcast_to(np.asarray(L0_conv_w_conv).reshape(1, K * N), (P, K * N))
    w_up = by_channel(L0_conv_w_up).reshape(P, TILES, 2)
    w_guide = by_channel(np.asarray(L1_conv_w_guide).T)
    w_fuse = by_channel(L1_conv_w_fuse).transpose(2, 1, 0)
    bn = np.stack([by_channel(v) for v in (L1_conv_bn_gamma, L1_conv_bn_beta, L1_conv_bn_mean,
                                           L1_conv_bn_var)], axis=1)
    arrays = {"x": x, "w_down": w_down, "w_conv": w_conv, "w_up": w_up, "w_guide": w_guide,
              "w_fuse": w_fuse, "bn": bn, "consts": shape_constants()}
    arrays = {k: np.ascontiguousarray(v) for k, v in arrays.items()}
    nc = bacc.Bacc("TRN2", target_bir_lowering=False, num_devices=1)
    args = [nc.dram_tensor(k, v.shape, mybir.dt.from_np(v.dtype), kind="ExternalInput").ap()
            for k, v in arrays.items()]
    args.append(nc.dram_tensor("out", (B, CH, H, W), F32, kind="ExternalOutput").ap())
    build(nc, *args)
    r = run_bass_kernel_spmd(nc, [arrays], core_ids=[0])
    return r.results[0]["out"]
```
